# Optimizing a Trainium2 kernel written in Bass

```python
import numpy as np
import jax
import jax.numpy as jnp

def _softmax(x, axis=-1):
    return jax.nn.softmax(x, axis=axis)

def _gelu(x):
    return jax.nn.gelu(x, approximate=True)

def _silu(x):
    return jax.nn.silu(x)

def _sigmoid(x):
    return jax.nn.sigmoid(x)

def _layernorm(x, axis=-1, eps=1e-05):
    m = jnp.mean(x, axis=axis, keepdims=True)
    v = jnp.var(x, axis=axis, keepdims=True)
    return (x - m) / jnp.sqrt(v + eps)

def _scatter_add(tgt, idx, src, axis=0):
    return tgt.at[idx].add(src)

def _segment_sum(src, seg, n):
    return jax.ops.segment_sum(src, seg, n)
kernel_name = 'mk_conv_preact_d4_conv_nchw2048_r4_1588b6'

def setup_inputs(seed: int=0):
    np.random.seed(seed)
    _w = jnp.asarray

    def _rec_inputs():
        import jax
        import jax.numpy as jnp
        _gk = jax.random.key(seed)
        x = -0.0003929 + 0.9999 * jax.random.normal(jax.random.fold_in(_gk, 1), (4, 512, 16, 32), jnp.float32)
        return x
    x = _rec_inputs()

    def _L0_conv_setup():
        import jax, jax.numpy as jnp
        import numpy as np
        B, T, H, DH = (4, 512, 16, 32)
        D = H * DH
        F = 1024
        E = 8
        TOP_K = 2
        key = jax.random.key(seed)
        ks = jax.random.split(key, 5)
        s_in = 1.0 / np.sqrt(D)
        s_f = 1.0 / np.sqrt(F)
        return {'stm': jax.random.normal(ks[0], (B, T, H, DH), dtype=jnp.float32), 'gate_w': jax.random.normal(ks[1], (E, D), dtype=jnp.float32) * s_in, 'w1': jax.random.normal(ks[2], (E, F, D), dtype=jnp.float32) * s_in, 'w2': jax.random.normal(ks[3], (E, D, F), dtype=jnp.float32) * s_f, 'w3': jax.random.normal(ks[4], (E, F, D), dtype=jnp.float32) * s_in}
    _L0_conv_all = _L0_conv_setup()
    _L0_conv_in = {k: v for k, v in _L0_conv_all.items() if k in ('gate_w', 'w1', 'w2', 'w3')}
    del _L0_conv_all

    def _L1_conv_setup():
        import jax, jax.numpy as jnp
        import numpy as np
        B, L, H, D = (4, 512, 16, 32)
        KERNEL_SIZES = (3, 7, 15)
        C = H * D

        def _causal_dwconv(x_flat, w):
            k = w.shape[-1]
            return jax.lax.conv_general_dilated(x_flat, w, window_strides=(1,), padding=[(k - 1, 0)], dimension_numbers=('NCH', 'OIH', 'NCH'), feature_group_count=x_flat.shape[1])
        key = jax.random.key(seed)
        k0, k1, k2, k3, k4 = jax.random.split(key, 5)
        x = jax.random.normal(k0, (B, L, H, D), dtype=jnp.float32)
        w3 = jax.random.normal(k1, (C, 1, 3), dtype=jnp.float32) * 0.02
        w7 = jax.random.normal(k2, (C, 1, 7), dtype=jnp.float32) * 0.02
        w15 = jax.random.normal(k3, (C, 1, 15), dtype=jnp.float32) * 0.02
        bound = 1.0 / np.sqrt(3 * D)
        w_mix = jax.random.uniform(k4, (D, 3 * D), dtype=jnp.float32, minval=-bound, maxval=bound)
        return {'x': x, 'w3': w3, 'w7': w7, 'w15': w15, 'w_mix': w_mix}
    _L1_conv_all = _L1_conv_setup()
    _L1_conv_in = {k: v for k, v in _L1_conv_all.items() if k in ('w3', 'w7', 'w15', 'w_mix')}
    del _L1_conv_all

    def _L2_conv_setup():
        import jax, jax.numpy as jnp
        import numpy as np
        B, L, H, D = (4, 512, 16, 32)
        KERNEL_SIZES = (3, 7, 15)
        C = H * D

        def _causal_dwconv(x_flat, w):
            k = w.shape[-1]
            return jax.lax.conv_general_dilated(x_flat, w, window_strides=(1,), padding=[(k - 1, 0)], dimension_numbers=('NCH', 'OIH', 'NCH'), feature_group_count=x_flat.shape[1])
        key = jax.random.key(seed)
        k0, k1, k2, k3, k4 = jax.random.split(key, 5)
        x = jax.random.normal(k0, (B, L, H, D), dtype=jnp.float32)
        w3 = jax.random.normal(k1, (C, 1, 3), dtype=jnp.float32) * 0.02
        w7 = jax.random.normal(k2, (C, 1, 7), dtype=jnp.float32) * 0.02
        w15 = jax.random.normal(k3, (C, 1, 15), dtype=jnp.float32) * 0.02
        bound = 1.0 / np.sqrt(3 * D)
        w_mix = jax.random.uniform(k4, (D, 3 * D), dtype=jnp.float32, minval=-bound, maxval=bound)
        return {'x': x, 'w3': w3, 'w7': w7, 'w15': w15, 'w_mix': w_mix}
    _L2_conv_all = _L2_conv_setup()
    _L2_conv_in = {k: v for k, v in _L2_conv_all.items() if k in ('w3', 'w7', 'w15', 'w_mix')}
    del _L2_conv_all

    def _L3_conv_setup():
        import jax, jax.numpy as jnp
        import numpy as np
        B, L, H, D = (4, 512, 16, 32)
        KERNEL_SIZES = (3, 7, 15)
        C = H * D

        def _causal_dwconv(x_flat, w):
            k = w.shape[-1]
            return jax.lax.conv_general_dilated(x_flat, w, window_strides=(1,), padding=[(k - 1, 0)], dimension_numbers=('NCH', 'OIH', 'NCH'), feature_group_count=x_flat.shape[1])
        key = jax.random.key(seed)
        k0, k1, k2, k3, k4 = jax.random.split(key, 5)
        x = jax.random.normal(k0, (B, L, H, D), dtype=jnp.float32)
        w3 = jax.random.normal(k1, (C, 1, 3), dtype=jnp.float32) * 0.02
        w7 = jax.random.normal(k2, (C, 1, 7), dtype=jnp.float32) * 0.02
        w15 = jax.random.normal(k3, (C, 1, 15), dtype=jnp.float32) * 0.02
        bound = 1.0 / np.sqrt(3 * D)
        w_mix = jax.random.uniform(k4, (D, 3 * D), dtype=jnp.float32, minval=-bound, maxval=bound)
        return {'x': x, 'w3': w3, 'w7': w7, 'w15': w15, 'w_mix': w_mix}
    _L3_conv_all = _L3_conv_setup()
    _L3_conv_in = {k: v for k, v in _L3_conv_all.items() if k in ('w3', 'w7', 'w15', 'w_mix')}
    del _L3_conv_all
    return {'x': x, 'L0_conv_gate_w': _L0_conv_in['gate_w'], 'L0_conv_w1': _L0_conv_in['w1'], 'L0_conv_w2': _L0_conv_in['w2'], 'L0_conv_w3': _L0_conv_in['w3'], 'L1_conv_w3': _L1_conv_in['w3'], 'L1_conv_w7': _L1_conv_in['w7'], 'L1_conv_w15': _L1_conv_in['w15'], 'L1_conv_w_mix': _L1_conv_in['w_mix'], 'L2_conv_w3': _L2_conv_in['w3'], 'L2_conv_w7': _L2_conv_in['w7'], 'L2_conv_w15': _L2_conv_in['w15'], 'L2_conv_w_mix': _L2_conv_in['w_mix'], 'L3_conv_w3': _L3_conv_in['w3'], 'L3_conv_w7': _L3_conv_in['w7'], 'L3_conv_w15': _L3_conv_in['w15'], 'L3_conv_w_mix': _L3_conv_in['w_mix']}

def reference(x, L0_conv_gate_w, L0_conv_w1, L0_conv_w2, L0_conv_w3, L1_conv_w3, L1_conv_w7, L1_conv_w15, L1_conv_w_mix, L2_conv_w3, L2_conv_w7, L2_conv_w15, L2_conv_w_mix, L3_conv_w3, L3_conv_w7, L3_conv_w15, L3_conv_w_mix):
    import jax
    import jax.numpy as jnp

    def _L0_conv_ref(stm, gate_w, w1, w2, w3):
        import jax, jax.numpy as jnp
        import numpy as np
        B, T, H, DH = (4, 512, 16, 32)
        D = H * DH
        F = 1024
        E = 8
        TOP_K = 2
        b, t, h, dh = stm.shape
        d = h * dh
        x = stm.reshape(b * t, d)
        logits = x @ gate_w.T
        top_logit, top_idx = jax.lax.top_k(logits, TOP_K)
        gw = jax.nn.softmax(top_logit.astype(jnp.float32), axis=1).astype(x.dtype)
        out = jnp.zeros_like(x)
        n_expert = w1.shape[0]
        for e in range(n_expert):
            we = jnp.sum(jnp.where(top_idx == e, gw, jnp.zeros_like(gw)), axis=1)
            gate = jax.nn.silu(x @ w1[e].T)
            up = x @ w3[e].T
            y = gate * up @ w2[e].T
            out = out + we[:, None] * y
        return out.reshape(b, t, h, dh)

    def _L1_conv_ref(x, w3, w7, w15, w_mix):
        import jax, jax.numpy as jnp
        import numpy as np
        B, L, H, D = (4, 512, 16, 32)
        KERNEL_SIZES = (3, 7, 15)
        C = H * D

        def _causal_dwconv(x_flat, w):
            k = w.shape[-1]
            return jax.lax.conv_general_dilated(x_flat, w, window_strides=(1,), padding=[(k - 1, 0)], dimension_numbers=('NCH', 'OIH', 'NCH'), feature_group_count=x_flat.shape[1])
        b, l, h, d = x.shape
        n_scales = 3
        x_flat = x.reshape(b, l, h * d).transpose(0, 2, 1)
        outs = [_causal_dwconv(x_flat, w) for w in (w3, w7, w15)]
        y = jnp.concatenate(outs, axis=1)
        y = y.reshape(b, h, n_scales * d, l).transpose(0, 3, 1, 2)
        return jnp.einsum('blhm,dm->blhd', y, w_mix)

    def _L2_conv_ref(x, w3, w7, w15, w_mix):
        import jax, jax.numpy as jnp
        import numpy as np
        B, L, H, D = (4, 512, 16, 32)
        KERNEL_SIZES = (3, 7, 15)
        C = H * D

        def _causal_dwconv(x_flat, w):
            k = w.shape[-1]
            return jax.lax.conv_general_dilated(x_flat, w, window_strides=(1,), padding=[(k - 1, 0)], dimension_numbers=('NCH', 'OIH', 'NCH'), feature_group_count=x_flat.shape[1])
        b, l, h, d = x.shape
        n_scales = 3
        x_flat = x.reshape(b, l, h * d).transpose(0, 2, 1)
        outs = [_causal_dwconv(x_flat, w) for w in (w3, w7, w15)]
        y = jnp.concatenate(outs, axis=1)
        y = y.reshape(b, h, n_scales * d, l).transpose(0, 3, 1, 2)
        return jnp.einsum('blhm,dm->blhd', y, w_mix)

    def _L3_conv_ref(x, w3, w7, w15, w_mix):
        import jax, jax.numpy as jnp
        import numpy as np
        B, L, H, D = (4, 512, 16, 32)
        KERNEL_SIZES = (3, 7, 15)
        C = H * D

        def _causal_dwconv(x_flat, w):
            k = w.shape[-1]
            return jax.lax.conv_general_dilated(x_flat, w, window_strides=(1,), padding=[(k - 1, 0)], dimension_numbers=('NCH', 'OIH', 'NCH'), feature_group_count=x_flat.shape[1])
        b, l, h, d = x.shape
        n_scales = 3
        x_flat = x.reshape(b, l, h * d).transpose(0, 2, 1)
        outs = [_causal_dwconv(x_flat, w) for w in (w3, w7, w15)]
        y = jnp.concatenate(outs, axis=1)
        y = y.reshape(b, h, n_scales * d, l).transpose(0, 3, 1, 2)
        return jnp.einsum('blhm,dm->blhd', y, w_mix)

    def _gn(v, G=32, eps=1e-05):
        B_, C_, H_, W_ = v.shape
        g = v.reshape(B_, G, C_ // G, H_, W_)
        m = jnp.mean(g, axis=(2, 3, 4), keepdims=True)
        s = jnp.var(g, axis=(2, 3, 4), keepdims=True)
        return ((g - m) / jnp.sqrt(s + eps)).reshape(v.shape)

    def _ln_c(v, eps=1e-06):
        m = jnp.mean(v, axis=1, keepdims=True)
        s = jnp.var(v, axis=1, keepdims=True)
        return (v - m) / jnp.sqrt(s + eps)

    def _ln_t(v, eps=1e-05):
        m = jnp.mean(v, axis=-1, keepdims=True)
        s = jnp.var(v, axis=-1, keepdims=True)
        return (v - m) / jnp.sqrt(s + eps)

    def _to_tokens(v):
        B_, C_, H_, W_ = v.shape
        return v.reshape(B_, C_, H_ * W_).transpose(0, 2, 1)

    def _from_tokens(t, like):
        B_, C_, H_, W_ = like.shape
        return t.transpose(0, 2, 1).reshape(B_, C_, H_, W_)
    x = x + _L0_conv_ref(_gn(x), L0_conv_gate_w, L0_conv_w1, L0_conv_w2, L0_conv_w3)
    x = x + _L1_conv_ref(_gn(x), L1_conv_w3, L1_conv_w7, L1_conv_w15, L1_conv_w_mix)
    x = x + _L2_conv_ref(_gn(x), L2_conv_w3, L2_conv_w7, L2_conv_w15, L2_conv_w_mix)
    x = x + _L3_conv_ref(_gn(x), L3_conv_w3, L3_conv_w7, L3_conv_w15, L3_conv_w_mix)
    return x

_drawn_inputs = setup_inputs


def setup_inputs(seed=0):
    import zlib

    import numpy as np

    out = dict(_drawn_inputs(seed))
    spreads = {}
    factors = {'L1_conv_w3': 5.098,
     'L1_conv_w7': 3.57,
     'L2_conv_w3': 5.104,
     'L2_conv_w7': 3.575,
     'L3_conv_w3': 5.106,
     'L3_conv_w7': 3.576}
    for name, (base, spread) in spreads.items():
        noise = np.random.default_rng([zlib.crc32(name.encode()), seed]).standard_normal(out[name].shape)
        drawn = base * np.exp(spread * noise) if base else spread * noise
        out[name] = jnp.asarray(drawn.astype(out[name].dtype))
    for name, factor in factors.items():
        out[name] = (out[name] * factor).astype(out[name].dtype)
    return out
```

```python
import concourse.bass as bass
from concourse import mybir
from contextlib import ExitStack

P = 128
BATCH, SEQ, D, F, E = 4, 512, 512, 1024, 8
QUARTERS = SEQ // P
TILES = BATCH * QUARTERS
TOKENS = BATCH * SEQ
TOP_K = 2
KD = D // P
KF = F // P
GROUP = SEQ // 32
GROUP_LANES = GROUP // QUARTERS
EPS = 1e-5
MAX_BLOCKS = (TOP_K * TOKENS + E * (P - 1)) // P
META = 4
ROW = D + META
LOW = -3.0e38
FREE = 1

LAYERS, HEADS, HD = 3, 16, 32
SCALES = (3, 7, 15)
HEAD_IN = len(SCALES) * HD
PHASES = QUARTERS
PAIR = 2
PT = PAIR * QUARTERS
LEAD = 4
CHUNKS = 8
XW = D + 64


def head_place(h):
    start = HEAD_IN * h % D
    if start % P <= P - HEAD_IN:
        return start // P, start % P
    return D // P + (start - 64) // P, (start - 64) % P


def head_taps(h):
    return SCALES[min((HEAD_IN * h + HEAD_IN - 1) // D, 2)]


CHUNK_HEADS = [[h for h in range(HEADS) if head_place(h)[0] == c] for c in range(CHUNKS)]
ORDER = [h for hs in CHUNK_HEADS for h in hs]
MIX_AT, _at = {}, 0
for _h in range(HEADS):
    MIX_AT[_h] = _at
    _at += (head_taps(_h) + 2 * (PHASES - 1)) * HD
MIX_COLS = _at
TAPS = max(SCALES)
MIX_MAX = TAPS * HD


def build(nc, x, gate_wT, w13T, w2T, taps, mixT, out):
    f32, f32r, i32, u32 = mybir.dt.float32, mybir.dt.float32r, mybir.dt.int32, mybir.dt.uint32
    ALU, ACT, AX = mybir.AluOpType, mybir.ActivationFunctionType, mybir.AxisListType

    slots_x = nc.dram_tensor("slots_x", [(MAX_BLOCKS + 2) * P, ROW], f32).ap()
    acc = nc.dram_tensor("acc", [TOKENS + P, D], f32).ap()
    with nc.sbuf_tensor("ident", [P, P], f32) as ident, nc.sbuf_tensor("group_mean", [P, P], f32) as group_mean:
        experts_part(nc, x, gate_wT, w13T, w2T, slots_x, acc, ident, group_mean)
        conv_part(nc, acc, taps, mixT, out, ident, group_mean)


def wait_apart(eng, semaphore, value, counter):
    eng.wait_ge(semaphore, value)
    eng.sem_inc(counter, 1)


def experts_part(nc, x, gate_wT, w13T, w2T, slots_x, acc, ident, group_mean):
    f32, f32r, i32, u32 = mybir.dt.float32, mybir.dt.float32r, mybir.dt.int32, mybir.dt.uint32
    ALU, ACT, AX = mybir.AluOpType, mybir.ActivationFunctionType, mybir.AxisListType
    x_rows = x.rearrange("b (p q) h w -> b p q (h w)", q=QUARTERS)

    with ExitStack() as ctx:
        def sb(name, shape, dt=f32):
            return ctx.enter_context(nc.sbuf_tensor(name, shape, dt))

        def ps(name, shape):
            return ctx.enter_context(nc.psum_tensor(name, shape, f32))

        def sem(name):
            return ctx.enter_context(nc.semaphore(name))

        w13_raw = sb("w13_raw", [P, KD, 2, F])
        w13_hi = sb("w13_hi", [P, KD, 2, F], f32r)
        w13_lo = sb("w13_lo", [P, KD, 2, F], f32r)
        w2_raw = sb("w2_raw", [P, KF, D])
        w2_hi = sb("w2_hi", [P, KF, D], f32r)
        w2_lo = sb("w2_lo", [P, KF, D], f32r)
        rows = sb("rows", [P, TILES, ROW])
        block_row = sb("block_row", [P, D])
        xT_hi = sb("xT_hi", [P, KD, P], f32r)
        xT_lo = sb("xT_lo", [P, KD, P], f32r)
        silu = sb("silu", [P, F])
        hidden = sb("hidden", [P, F])
        hT_hi = sb("hT_hi", [P, KF, P], f32r)
        hT_lo = sb("hT_lo", [P, KF, P], f32r)
        y_row = sb("y_row", [P, D])
        meta = sb("meta", [P, META])
        my_slot = sb("my_slot", [P, 1])
        weight = sb("weight", [P, 1])
        before = sb("before", [P, P])
        ones = sb("ones", [P, P])
        pad_row = sb("pad_row", [P, ROW])
        gate_sb = sb("gate_sb", [P, KD, E])
        gate_xT = w2_raw[:, :, :].rearrange("p (s a) n -> p s (a n)", s=4)
        bn = sb("bn", [P, BATCH, QUARTERS, 6])
        mv = sb("mv", [P, BATCH, 2])
        gmv = sb("gmv", [P, BATCH, 2])
        dev = sb("dev", [P, BATCH, 2])
        rstd = sb("rstd", [P, BATCH, 4])
        ids = sb("ids", [P, TILES], i32)
        pad_id = sb("pad_id", [P, 1], i32)
        rev = sb("rev", [P, E])
        thresholds = sb("thresholds", [P, TILES - 1])
        best = sb("best", [P, 8, TILES])
        over = sb("over", [P, E, TILES - 1])
        lg, eq, score, pick1, pick2, lg2, mask, slot = (
            hidden[:, n * P:(n + 1) * P].rearrange("p (i e) -> p i e", e=E) for n in range(8))
        restart, totals, running = (
            silu[:, n * P:(n + 1) * P].rearrange("p (e i) -> p e i", i=TILES) for n in range(3))
        nblocks = sb("nblocks", [P, 4, E])
        slot_id = sb("slot_id", [P, TOP_K, TILES], i32)
        table = sb("table", [1, 16], i32)

        xT_ps = ps("xT_ps", [P, 512])
        gate_ps = ps("gate_ps", [P, 2, 512])
        up_ps = ps("up_ps", [P, 2, 512])
        hT_ps = ps("hT_ps", [P, KF, P])
        y_ps = ps("y_ps", [P, 512])

        x_in = [sem(f"x_in{b}") for b in range(BATCH)]
        gate_in = sem("gate_in")
        acc_ready = sem("acc_ready")
        consts = sem("consts")
        pool_step = sem("pool_step")
        d_step = sem("d_step")
        stat_ps = sem("stat_ps")
        normed = sem("normed")
        rooted = sem("rooted")
        gxT_ps = sem("gxT_ps")
        gxT_sb = sem("gxT_sb")
        logits = sem("logits")
        ranks = sem("ranks")
        mask_ready = sem("mask_ready")
        gap_ready = sem("gap_ready")
        exped = sem("exped")
        table_ready = sem("table_ready")
        pads_in = sem("pads_in")
        rows_ready = sem("rows_ready")
        scattered = sem("scattered")
        w13_in = [sem(f"w13_in{k}") for k in range(KD)]
        w2_in = [sem(f"w2_in{k}") for k in range(2)]
        w13_hi_ok = sem("w13_hi_ok")
        w13_ok = sem("w13_ok")
        w2_hi_ok = sem("w2_hi_ok")
        w2_ok = sem("w2_ok")
        row_in = sem("row_in")
        xT_done = sem("xT_done")
        xT_hi_ok = sem("xT_hi_ok")
        xT_ok = sem("xT_ok")
        up_done = sem("up_done")
        silu_ok = sem("silu_ok")
        hidden_ok = sem("hidden_ok")
        hT_done = sem("hT_done")
        hT_hi_ok = sem("hT_hi_ok")
        hT_ok = sem("hT_ok")
        down_done = sem("down_done")
        y_ok = sem("y_ok")
        meta_in = sem("meta_in")
        weight_ok = sem("weight_ok")
        w_step = sem("w_step")
        added = sem("added")
        passed = sem("passed")

        block = ctx.enter_context(nc.Block(name="experts"))

        def load_w13(eng, e, k):
            eng.dma_start(w13_raw[:, k], w13T[bass.ds(e, 1), k].rearrange("o p t n -> (o p) t n"))\
               .then_inc(w13_in[k], 16)

        def load_w2(eng, e, half):
            k = slice(half * KF // 2, (half + 1) * KF // 2)
            eng.dma_start(w2_raw[:, k], w2T[bass.ds(e, 1), :, k].rearrange("o p t n -> (o p) t n"))\
               .then_inc(w2_in[half], 16)

        def last_block_of(eng, e):
            return eng.value_load(table[0:1, bass.ds(e, 1)], min_val=0, max_val=MAX_BLOCKS - 1)

        def all_blocks(eng, new_expert, body, after_first):
            def one_expert(e, first, last):
                new_expert(e, first)
                body(e, first, True)
                after_first(e, first)
                with eng.If(last > first):
                    with eng.Fori(first + 1, last + 1) as g:
                        body(e, g, False)
            one_expert(0, 0, last_block_of(eng, 0))
            with eng.Fori(1, E) as e:
                one_expert(e, last_block_of(eng, e - 1) + 1, last_block_of(eng, e))

        @block.sync
        def _(sp):
            for b in range(BATCH):
                sp.dma_start(rows[:, b * QUARTERS:(b + 1) * QUARTERS, 0:D], x_rows[b]).then_inc(x_in[b], 16)
            for k in range(KD):
                load_w13(sp, 0, k)
            sp.wait_ge(table_ready, 1)
            sp.wait_ge(consts, 2)
            with sp.Fori(0, E) as e:
                last = last_block_of(sp, e)
                sp.dma_start(slots_x[bass.ds(last * P, P), :], pad_row[:, :]).then_inc(pads_in, 16)
            end = last_block_of(sp, E - 1) + 1
            sp.dma_start(slots_x[bass.ds(end * P, P), :], pad_row[:, :]).then_inc(pads_in, 16)
            sp.wait_ge(logits, TILES)
            for half in range(2):
                load_w2(sp, 0, half)
            with sp.Fori(1, E) as e:
                for k in range(KD):
                    sp.wait_ge(w13_ok, (e - 1) * KD + k + 1)
                    load_w13(sp, e, k)
                for half in range(2):
                    sp.wait_ge(w2_ok, (e - 1) * 2 + half + 1)
                    load_w2(sp, e, half)

        @block.gpsimd
        def _(pool):
            steps = [0]

            def step(ins):
                steps[0] += 1
                ins.then_inc(pool_step, 1)
                pool.wait_ge(pool_step, steps[0])

            step(nc.gpsimd.memset(ident[:, :], 0.0))
            step(nc.gpsimd.affine_select(out=ident[:, :], in_=ident[:, :], compare_op=ALU.not_equal, fill=1.0,
                                         base=0, pattern=[[-1, P]], channel_multiplier=1))
            step(nc.gpsimd.memset(group_mean[:, :], 1.0 / GROUP_LANES))
            blocks = group_mean[:, :].rearrange("p (a c) -> p a c", c=GROUP_LANES)
            step(nc.gpsimd.affine_select(out=blocks, in_=blocks, compare_op=ALU.is_ge, fill=0.0, base=0,
                                         pattern=[[-GROUP_LANES, P // GROUP_LANES], [0, GROUP_LANES]],
                                         channel_multiplier=1))
            step(nc.gpsimd.affine_select(out=blocks, in_=blocks, compare_op=ALU.is_ge, fill=0.0,
                                         base=GROUP_LANES - 1,
                                         pattern=[[GROUP_LANES, P // GROUP_LANES], [0, GROUP_LANES]],
                                         channel_multiplier=-1))
            nc.gpsimd.memset(ones[:, :], 1.0).then_inc(consts, 1)
            step(nc.gpsimd.memset(before[:, :], 1.0))
            step(nc.gpsimd.affine_select(out=before[:, :], in_=before[:, :], compare_op=ALU.is_ge, fill=0.0,
                                         base=-1, pattern=[[1, P]], channel_multiplier=-1))
            step(nc.gpsimd.memset(pad_row[:, :], 0.0))
            step(nc.gpsimd.memset(pad_row[:, D + 1:D + 2], -1.0))
            step(nc.gpsimd.iota(pad_id[:, :], pattern=[[0, 1]], base=TOKENS, channel_multiplier=1))
            step(nc.gpsimd.tensor_copy(pad_row[:, D:D + 1].bitcast(i32), pad_id[:, :]))
            step(nc.gpsimd.iota(ids[:, :].rearrange("p (b q) -> p b q", q=QUARTERS),
                                pattern=[[SEQ, BATCH], [1, QUARTERS]], base=0, channel_multiplier=QUARTERS))
            step(nc.gpsimd.iota(rev[:, :], pattern=[[-1, E]], base=E, channel_multiplier=0,
                                allow_small_or_imprecise_dtypes=True))
            step(nc.gpsimd.iota(thresholds[:, :], pattern=[[P, TILES - 1]], base=P, channel_multiplier=0,
                                allow_small_or_imprecise_dtypes=True))
            step(nc.gpsimd.iota(my_slot[:, :], pattern=[[0, 1]], base=0, channel_multiplier=1,
                                allow_small_or_imprecise_dtypes=True))
            step(nc.gpsimd.memset(restart[:, :, :], 1.0))
            nc.gpsimd.memset(restart[:, :, 0:1], 0.0).then_inc(consts, 1)
            pool.dma_start(acc[0:TOKENS, :].rearrange("(p a) n -> p (a n)", p=P),
                           x.rearrange("b (p a) h w -> (b p) (a h w)", a=TOKENS // P)).then_inc(acc_ready, 16)
            pool.dma_start(acc[TOKENS:TOKENS + P, :], pad_row[:, 0:D]).then_inc(acc_ready, 16)

            pool.wait_ge(rows_ready, 1)
            pool.wait_ge(pads_in, 16 * (E + 1))
            for j in range(TOP_K):
                for i in range(TILES):
                    pool.indirect_dma_start(
                        out=slots_x[:, :], out_offset=bass.IndirectOffsetOnAxis(slot_id[:, j, i:i + 1].bitcast(u32), 0),
                        in_=rows[:, i, :], in_offset=None).then_inc(scattered, 16)
            pool.wait_ge(scattered, 16 * TOP_K * TILES)
            pool.dma_start(block_row[:, :], slots_x[0:P, 0:D]).then_inc(row_in, 16)
            pool.wait_ge(acc_ready, 32)

            def add_block(g):
                wait_apart(pool, y_ok, g + 1 + FREE, passed)
                pool.indirect_dma_start(
                    out=acc[:, :], out_offset=bass.IndirectOffsetOnAxis(meta[:, 0:1].bitcast(u32), 0),
                    in_=y_row[:, :], in_offset=None, compute_op=ALU.add).then_inc(added, 16)
                wait_apart(pool, added, 16 * (g + 1), passed)

            def weigh_block(g):
                pool.dma_start(meta[:, :], slots_x[bass.ds(g * P, P), D:ROW]).then_inc(meta_in, 16)
                wait_apart(pool, meta_in, 16 * (g + 1), passed)
                nc.gpsimd.tensor_scalar(weight[:, :], meta[:, 1:2], my_slot[:, :], meta[:, 3:4],
                                        ALU.is_equal, ALU.mult).then_inc(w_step, 1)
                wait_apart(pool, w_step, 2 * g + 1, passed)
                nc.gpsimd.tensor_scalar(my_slot[:, :], my_slot[:, :], float(P), None, ALU.add).then_inc(w_step, 1)
                nc.gpsimd.tensor_tensor(weight[:, :], weight[:, :], meta[:, 2:3], ALU.add).then_inc(weight_ok, 1)
                wait_apart(pool, w_step, 2 * g + 2, passed)
                wait_apart(pool, weight_ok, g + 1, passed)

            def body(e, g, first):
                pool.wait_ge(xT_done, g + 1)
                pool.dma_start(block_row[:, :], slots_x[bass.ds((g + 1) * P, P), 0:D]).then_inc(row_in, 16)
                if isinstance(g, int):
                    return
                with pool.If(g > 1):
                    add_block(g - 2)
                weigh_block(g - 1)

            all_blocks(pool, lambda e, g: None, body, lambda e, g: None)
            g = last_block_of(pool, E - 1)
            add_block(g - 1)
            weigh_block(g)
            add_block(g)
            pool.wait_ge(row_in, 16 * (g + 2))

        @block.scalar
        def _(act):
            act.sem_inc(y_ok, FREE)
            act.dma_start(gate_sb[:, :, :], gate_wT).then_inc(gate_in, 16)
            for b in range(BATCH):
                act.wait_ge(rooted, 2 * b + 1)
                nc.scalar.activation(rstd[:, b, 1:2], rstd[:, b, 0:1], ACT.Sqrt).then_inc(rooted, 1)
                for i in range(b * QUARTERS, (b + 1) * QUARTERS):
                    act.wait_ge(gxT_ps, i + 1)
                    if i >= 4:
                        act.wait_ge(logits, i - 3)
                    nc.scalar.activation(gate_xT[:, i % 4, 0:512], gate_ps[:, i % 2, :], ACT.Copy).then_inc(gxT_sb, 1)
            act.wait_ge(gap_ready, 1)
            nc.scalar.activation(best[:, 3, :], best[:, 2, :], ACT.Exp).then_inc(exped, 1)

            def split_w13(e, g0):
                for k in range(KD):
                    act.wait_ge(w13_in[k], 16 * (e + 1))
                    if not isinstance(e, int):
                        act.wait_ge(up_done, g0 * KD + (k + 1 - KD))
                    nc.scalar.activation(w13_hi[:, k], w13_raw[:, k], ACT.Copy).then_inc(w13_hi_ok, 1)

            def split_w2(e, g0):
                if not isinstance(e, int):
                    act.wait_ge(down_done, g0 + FREE)
                for half in range(2):
                    act.wait_ge(w2_in[half], 16 * (e + 1))
                    k = slice(half * KF // 2, (half + 1) * KF // 2)
                    nc.scalar.activation(w2_hi[:, k], w2_raw[:, k], ACT.Copy).then_inc(w2_hi_ok, 1)

            def xT_high(g):
                act.wait_ge(xT_done, g + 1)
                nc.scalar.activation(xT_hi[:, :, :].rearrange("p a n -> p (a n)"), xT_ps[:, :], ACT.Copy).then_inc(xT_hi_ok, 1)

            def hT_high(g):
                act.wait_ge(hT_done, g + 1)
                act.wait_ge(down_done, g + FREE)
                nc.scalar.activation(hT_hi[:, :, :], hT_ps[:, :, :], ACT.Copy).then_inc(hT_hi_ok, 1)

            def weigh_y(g):
                act.wait_ge(down_done, g + 1 + FREE)
                act.wait_ge(weight_ok, g + 1)
                nc.scalar.activation(y_row[:, :], y_ps[:, :], ACT.Copy, scale=weight[:, :]).then_inc(y_ok, 1)

            def body(e, g, first):
                if not isinstance(g, int):
                    with act.If(g > 1):
                        weigh_y(g - 2)
                    hT_high(g - 1)
                act.wait_ge(up_done, KD * (g + 1))
                if not isinstance(g, int):
                    act.wait_ge(hidden_ok, g)
                nc.scalar.activation(silu[:, :].rearrange("p (a n) -> p a n", a=2), gate_ps[:, :, :], ACT.Silu).then_inc(silu_ok, 1)
                xT_high(g + 1)

            act.wait_ge(table_ready, 1)
            xT_high(0)
            all_blocks(act, split_w13, body, split_w2)
            g = last_block_of(act, E - 1)
            weigh_y(g - 1)
            hT_high(g)
            weigh_y(g)

        @block.vector
        def _(dve):
            steps = [0]

            def step(ins):
                steps[0] += 1
                ins.then_inc(d_step, 1)
                dve.wait_ge(d_step, steps[0])

            def flush():
                dve.wait_ge(d_step, steps[0])

            def count(ins):
                steps[0] += 1
                ins.then_inc(d_step, 1)

            for b in range(BATCH):
                dve.wait_ge(x_in[b], 16)
                for q in range(QUARTERS):
                    count(nc.vector.bn_stats(bn[:, b, q, :], rows[:, b * QUARTERS + q, 0:D]))
                flush()
                nc.vector.bn_aggr(mv[:, b, :], bn[:, b, :, :].rearrange("p q s -> p (q s)")).then_inc(normed, 1)
                dve.wait_ge(stat_ps, 2 * b + 1)
                step(nc.vector.tensor_copy(gmv[:, b, :], up_ps[:, 0, 2 * b:2 * b + 2]))
                step(nc.vector.tensor_scalar(dev[:, b, 0:1], mv[:, b, 0:1], gmv[:, b, 0:1], None, ALU.subtract))
                nc.vector.tensor_tensor(dev[:, b, 1:2], dev[:, b, 0:1], dev[:, b, 0:1], ALU.mult).then_inc(normed, 1)
                dve.wait_ge(stat_ps, 2 * b + 2)
                nc.vector.tensor_scalar(rstd[:, b, 0:1], up_ps[:, 1, b:b + 1], gmv[:, b, 1:2], EPS, ALU.add, ALU.add).then_inc(rooted, 1)
                dve.wait_ge(rooted, 2 * b + 2)
                step(nc.vector.reciprocal(rstd[:, b, 2:3], rstd[:, b, 1:2]))
                for q in range(QUARTERS):
                    r = rows[:, b * QUARTERS + q, 0:D]
                    nc.vector.tensor_scalar(r, r, gmv[:, b, 0:1], rstd[:, b, 2:3], ALU.subtract, ALU.mult).then_inc(normed, 1)

            bc = [P, TILES, E]
            dve.wait_ge(consts, 2)
            dve.wait_ge(logits, TILES)
            step(nc.vector.tensor_copy(lg[:, :, :].rearrange("p i e -> p (i e)"), y_ps[:, 0:TILES * E]))

            def pick(source, top, which, onehot):
                step(nc.vector.tensor_reduce(best[:, top, :], source, axis=AX.X, op=ALU.max))
                step(nc.vector.tensor_tensor(eq[:, :, :], source, best[:, top, :, None].to_broadcast(bc), ALU.is_equal))
                step(nc.vector.tensor_tensor(score[:, :, :], eq[:, :, :], rev[:, None, :].to_broadcast(bc), ALU.mult))
                step(nc.vector.tensor_reduce(best[:, which, :], score[:, :, :], axis=AX.X, op=ALU.max))
                step(nc.vector.tensor_tensor(onehot, score[:, :, :], best[:, which, :, None].to_broadcast(bc), ALU.is_equal))

            pick(lg[:, :, :], 0, 6, pick1[:, :, :])
            step(nc.vector.scalar_tensor_tensor(lg2[:, :, :], pick1[:, :, :], LOW, lg[:, :, :], ALU.mult, ALU.add))
            pick(lg2[:, :, :], 1, 7, pick2[:, :, :])
            nc.vector.tensor_tensor(mask[:, :, :], pick1[:, :, :], pick2[:, :, :], ALU.add).then_inc(mask_ready, 1)
            nc.vector.tensor_tensor(best[:, 2, :], best[:, 1, :], best[:, 0, :], ALU.subtract).then_inc(gap_ready, 1)
            dve.wait_ge(ranks, 2)
            step(nc.vector.tensor_copy(totals[:, :, :], hT_ps[:, 4, :].rearrange("p (i e) -> p e i", e=E)))
            step(nc.vector.tensor_tensor_scan(running[:, :, :].rearrange("p e i -> p (e i)"),
                                              restart[:, :, :].rearrange("p e i -> p (e i)"),
                                              totals[:, :, :].rearrange("p e i -> p (e i)"), 0.0, ALU.mult, ALU.add))
            step(nc.vector.tensor_tensor(over[:, :, :], running[:, :, TILES - 1:TILES].to_broadcast([P, E, TILES - 1]),
                                         thresholds[:, None, :].to_broadcast([P, E, TILES - 1]), ALU.is_gt))
            step(nc.vector.tensor_reduce(nblocks[:, 0, :], over[:, :, :], axis=AX.X, op=ALU.add))
            step(nc.vector.tensor_scalar(nblocks[:, 0, :], nblocks[:, 0, :], 1.0, None, ALU.add))
            step(nc.vector.tensor_tensor_scan(nblocks[:, 1, :], ones[:, 0:E], nblocks[:, 0, :], 0.0, ALU.mult, ALU.add))
            step(nc.vector.tensor_tensor(nblocks[:, 2, :], nblocks[:, 1, :], nblocks[:, 0, :], ALU.subtract))
            nc.vector.tensor_scalar(table[0:1, 0:E], nblocks[0:1, 1, :], 1.0, None, ALU.subtract).then_inc(table_ready, 1)
            step(nc.vector.tensor_scalar(nblocks[:, 3, :], nblocks[:, 2, :], float(P), None, ALU.mult))
            step(nc.vector.tensor_tensor(running[:, :, :], running[:, :, :], totals[:, :, :], ALU.subtract))
            step(nc.vector.tensor_tensor(running[:, :, :], running[:, :, :], nblocks[:, 3, :, None].to_broadcast([P, E, TILES]), ALU.add))
            step(nc.vector.tensor_tensor(slot[:, :, :], hT_ps[:, 0, :].rearrange("p (i e) -> p i e", e=E),
                                         running[:, :, :].rearrange("p e i -> p i e"), ALU.add))
            for j, onehot in enumerate((pick1, pick2)):
                step(nc.vector.tensor_tensor(eq[:, :, :], slot[:, :, :], onehot[:, :, :], ALU.mult))
                step(nc.vector.tensor_reduce(best[:, 6 + j, :], eq[:, :, :], axis=AX.X, op=ALU.add))
                step(nc.vector.tensor_copy(slot_id[:, j, :], best[:, 6 + j, :]))
            dve.wait_ge(exped, 1)
            step(nc.vector.tensor_scalar(best[:, 4, :], best[:, 3, :], 1.0, None, ALU.add))
            step(nc.vector.reciprocal(best[:, 5, :], best[:, 4, :]))
            step(nc.vector.tensor_tensor(rows[:, :, D + 2], best[:, 3, :], best[:, 5, :], ALU.mult))
            count(nc.vector.tensor_tensor(rows[:, :, D + 3], best[:, 5, :], rows[:, :, D + 2], ALU.subtract))
            count(nc.vector.tensor_copy(rows[:, :, D + 1], best[:, 6, :]))
            count(nc.vector.tensor_copy(rows[:, :, D].bitcast(i32), ids[:, :]))
            flush()
            dve.sem_inc(rows_ready, 1)

            def split_w13(e, g0):
                for k in range(KD):
                    dve.wait_ge(w13_hi_ok, KD * e + (k + 1))
                    nc.vector.tensor_tensor(w13_lo[:, k], w13_raw[:, k], w13_hi[:, k].bitcast(f32),
                                            ALU.subtract).then_inc(w13_ok, 1)

            def split_w2(e, g0):
                for half in range(2):
                    dve.wait_ge(w2_hi_ok, 2 * e + (half + 1))
                    k = slice(half * KF // 2, (half + 1) * KF // 2)
                    nc.vector.tensor_tensor(w2_lo[:, k], w2_raw[:, k], w2_hi[:, k].bitcast(f32),
                                            ALU.subtract).then_inc(w2_ok, 1)

            def xT_low(g):
                dve.wait_ge(xT_hi_ok, g + 1)
                nc.vector.tensor_tensor(xT_lo[:, :, :].rearrange("p a n -> p (a n)"), xT_ps[:, :],
                                        xT_hi[:, :, :].rearrange("p a n -> p (a n)").bitcast(f32), ALU.subtract).then_inc(xT_ok, 1)

            def hT_low(g):
                dve.wait_ge(hT_hi_ok, g + 1)
                nc.vector.tensor_tensor(hT_lo[:, :, :], hT_ps[:, :, :], hT_hi[:, :, :].bitcast(f32),
                                        ALU.subtract).then_inc(hT_ok, 1)

            def body(e, g, first):
                if not isinstance(g, int):
                    hT_low(g - 1)
                dve.wait_ge(silu_ok, g + 1)
                if not isinstance(g, int):
                    dve.wait_ge(hT_done, g)
                nc.vector.tensor_tensor(hidden[:, :].rearrange("p (a n) -> p a n", a=2),
                                        silu[:, :].rearrange("p (a n) -> p a n", a=2), up_ps[:, :, :],
                                        ALU.mult).then_inc(hidden_ok, 1)
                xT_low(g + 1)

            dve.wait_ge(table_ready, 1)
            xT_low(0)
            all_blocks(dve, split_w13, body, split_w2)
            hT_low(last_block_of(dve, E - 1))

        def gate_logits(pe, i):
            pe.wait_ge(gxT_sb, i + 1)
            for k in range(KD):
                last = nc.tensor.matmul(y_ps[:, i * E:(i + 1) * E], gate_xT[:, i % 4, k * P:(k + 1) * P],
                                        gate_sb[:, k, :], start=(k == 0), stop=(k == KD - 1))
            last.then_inc(logits, 1)

        @block.tensor
        def _(pe):
            pe.sem_inc(down_done, FREE)
            pe.wait_ge(pool_step, 5)
            pe.wait_ge(gate_in, 16)
            seen = 0
            for b in range(BATCH):
                pe.wait_ge(normed, seen + 1)
                nc.tensor.matmul(up_ps[:, 0, 2 * b:2 * b + 2], group_mean[:, :], mv[:, b, :], start=True, stop=True).then_inc(stat_ps, 1)
                pe.wait_ge(normed, seen + 2)
                nc.tensor.matmul(up_ps[:, 1, b:b + 1], group_mean[:, :], dev[:, b, 1:2], start=True, stop=True).then_inc(stat_ps, 1)
                seen += 2
                for q in range(QUARTERS):
                    i = b * QUARTERS + q
                    seen += 1
                    pe.wait_ge(normed, seen)
                    if i >= 2:
                        pe.wait_ge(gxT_sb, i - 1)
                    for k in range(KD):
                        last = nc.tensor.transpose(gate_ps[:, i % 2, k * P:(k + 1) * P], rows[:, i, k * P:(k + 1) * P], ident[:, :])
                    last.then_inc(gxT_ps, 1)
                    if i:
                        gate_logits(pe, i - 1)
            gate_logits(pe, TILES - 1)
            pe.wait_ge(mask_ready, 1)
            pe.wait_ge(consts, 1)
            pe.wait_ge(pool_step, 7)
            nc.tensor.matmul(hT_ps[:, 0, :], before[:, :], mask[:, :, :].rearrange("p i e -> p (i e)"), start=True, stop=True).then_inc(ranks, 1)
            nc.tensor.matmul(hT_ps[:, 4, :], ones[:, :], mask[:, :, :].rearrange("p i e -> p (i e)"), start=True, stop=True).then_inc(ranks, 1)

            def transpose_rows(g):
                pe.wait_ge(row_in, 16 * (g + 1))
                for k in range(KD):
                    last = nc.tensor.transpose(xT_ps[:, k * P:(k + 1) * P], block_row[:, k * P:(k + 1) * P], ident[:, :])
                last.then_inc(xT_done, 1)

            def down(g, w2_count):
                pe.wait_ge(y_ok, g + FREE)
                pe.wait_ge(w2_ok, w2_count)
                pe.wait_ge(hT_ok, g + 1)
                for k in range(KF):
                    for a, b in ((hT_hi, w2_hi), (hT_hi, w2_lo), (hT_lo, w2_hi)):
                        last = nc.tensor.matmul(y_ps[:, :], a[:, k, :], b[:, k, :],
                                                start=(k == 0 and b is w2_hi and a is hT_hi),
                                                stop=(k == KF - 1 and a is hT_lo))
                last.then_inc(down_done, 1)

            def body(e, g, first):
                pe.wait_ge(xT_ok, g + 1)
                for k in range(KD):
                    pe.wait_ge(w13_ok, KD * e + (k + 1))
                    for a, b in ((xT_hi, w13_hi), (xT_hi, w13_lo), (xT_lo, w13_hi)):
                        for t, o in ((0, gate_ps), (1, up_ps)):
                            for n in range(2):
                                last = nc.tensor.matmul(o[:, n, :], a[:, k, :], b[:, k, t, n * 512:(n + 1) * 512],
                                                        start=(k == 0 and a is xT_hi and b is w13_hi),
                                                        stop=(k == KD - 1 and a is xT_lo))
                    last.then_inc(up_done, 1)
                transpose_rows(g + 1)
                if not isinstance(g, int):
                    down(g - 1, 2 * e if first else 2 * e + 2)
                pe.wait_ge(hidden_ok, g + 1)
                for k in range(KF):
                    last = nc.tensor.transpose(hT_ps[:, k, :], hidden[:, k * P:(k + 1) * P], ident[:, :])
                last.then_inc(hT_done, 1)

            pe.wait_ge(table_ready, 1)
            transpose_rows(0)
            all_blocks(pe, lambda e, g: None, body, lambda e, g: None)
            down(last_block_of(pe, E - 1), 2 * E)



def conv_part(nc, acc, taps, mixT, out, ident, group_mean):
    f32, f32r = mybir.dt.float32, mybir.dt.float32r
    ALU, ACT = mybir.AluOpType, mybir.ActivationFunctionType
    acc_rows = acc[0:TOKENS, :].rearrange("(b p q) n -> b p q n", p=P, q=QUARTERS)
    out_rows = out.rearrange("b (p q) h w -> b p q (h w)", q=QUARTERS)
    NORM_STEPS = 19

    with ExitStack() as ctx:
        def sb(name, shape, dt=f32):
            return ctx.enter_context(nc.sbuf_tensor(name, shape, dt))

        def ps(name, shape):
            return ctx.enter_context(nc.psum_tensor(name, shape, f32))

        def sem(name):
            return ctx.enter_context(nc.semaphore(name))

        tokens = sb("tokens", [P, TILES, D])
        norm = sb("norm", [P, PT, XW])
        ch_hi = [sb(f"ch_hi{i}", [P, PAIR, QUARTERS, LEAD + P], f32r) for i in range(2)]
        ch_lo = [sb(f"ch_lo{i}", [P, PAIR, QUARTERS, LEAD + P], f32r) for i in range(2)]
        mix_hi = sb("mix_hi", [P, MIX_COLS], f32r)
        mix_lo = sb("mix_lo", [P, MIX_COLS], f32r)
        product = [sb(f"product{i}", [P, MIX_MAX]) for i in range(4)]
        taps_sb = sb("taps_sb", [P, LAYERS + 1, HEADS, TAPS])
        mix_sb = sb("mix_sb", [P, LAYERS + 1, 2, HD])
        mixed = sb("mixed", [P, 2, PAIR * P])
        bn = sb("bn_c", [P, PAIR, QUARTERS, 6])
        mv = sb("mv_c", [P, PAIR, 2])
        gmv = sb("gmv_c", [P, PAIR, 2])
        dev = sb("dev_c", [P, PAIR])
        dev2 = sb("dev2_c", [P, PAIR])
        var = sb("var_c", [P, PAIR])
        std = sb("std_c", [P, PAIR])
        rstd = sb("rstd_c", [P, PAIR])

        chT_ps = ps("chT_ps", [P, PT, P])
        mixed_ps = [ps(f"mixed_ps{i}", [P, 512]) for i in range(2)]
        back_ps = ps("back_ps", [P, 2, PAIR, P])
        stat_ps = ps("stat_ps", [P, 512])
        stat2_ps = ps("stat2_ps", [P, 512])

        tokens_in = [sem(f"tokens_in{i}") for i in range(2)]
        taps_in = sem("taps_in")
        zeroed = sem("zeroed")
        norm_step = sem("norm_step")
        stat_done = sem("stat_done")
        root_ok = sem("root_ok")
        chT_done = sem("chT_done")
        ch_hi_ok = sem("ch_hi_ok")
        ch_ok = sem("ch_ok")
        head_done = sem("head_done")
        mixed_ok = sem("mixed_ok")
        back_done = sem("back_done")
        summed = sem("summed")
        product_ok = sem("product_ok")
        mix_hi_ok = sem("mix_hi_ok")
        mix_ok = sem("mix_ok")
        stored = sem("stored")
        passed = sem("passed_c")
        block = ctx.enter_context(nc.Block(name="convolutions"))

        def middle(t, h):
            at = MIX_AT[h] + (PHASES - 1) * HD
            return t[:, at:at + head_taps(h) * HD]

        @block.sync
        def _(sp):
            sp.dma_start(tokens[:, 0:QUARTERS, :], acc_rows[0]).then_inc(tokens_in[0], 16)
            sp.dma_start(tokens[:, QUARTERS:PT, :], acc_rows[1]).then_inc(tokens_in[0], 16)
            sp.dma_start(taps_sb[:, 0:LAYERS], taps).then_inc(taps_in, 16)
            sp.dma_start(mix_sb[:, 0:LAYERS], mixT).then_inc(taps_in, 16)
            for b in range(PAIR, BATCH):
                sp.dma_start(tokens[:, b * QUARTERS:(b + 1) * QUARTERS, :], acc_rows[b]).then_inc(tokens_in[1], 16)
            for pair in range(2):
                sp.wait_ge(summed, CHUNKS * (2 * (LAYERS - 1) + pair + 1) + FREE)
                for b in range(pair * PAIR, (pair + 1) * PAIR):
                    sp.dma_start(out_rows[b], tokens[:, b * QUARTERS:(b + 1) * QUARTERS, :]).then_inc(stored, 16)
            sp.wait_ge(stored, 16 * BATCH)

        @block.gpsimd
        def _(pool):
            for i in range(2):
                nc.gpsimd.memset(ch_hi[i][:, :, :, 0:LEAD].bitcast(f32), 0.0).then_inc(zeroed, 1)
                nc.gpsimd.memset(ch_lo[i][:, :, :, 0:LEAD].bitcast(f32), 0.0).then_inc(zeroed, 1)
            for h in ORDER:
                for t in (mix_hi, mix_lo):
                    k = head_taps(h)
                    for at in (MIX_AT[h], MIX_AT[h] + (PHASES - 1 + k) * HD):
                        nc.gpsimd.memset(t[:, at:at + (PHASES - 1) * HD].bitcast(f32), 0.0).then_inc(zeroed, 1)

        def layers(eng, stage):
            with eng.Fori(0, LAYERS) as l:
                for pair in range(2):
                    stage(l, pair)

        @block.scalar
        def _(act):
            def root(s):
                act.wait_ge(norm_step, NORM_STEPS * s + 14)
                nc.scalar.activation(std[:, :], var[:, :], ACT.Sqrt).then_inc(root_ok, 1)

            def high(s, c):
                act.wait_ge(chT_done, CHUNKS * s + (c + 1))
                nc.scalar.activation(ch_hi[c % 2][:, :, :, LEAD:].rearrange("p b q n -> p (b q) n"),
                                     chT_ps[:, :, :], ACT.Copy).then_inc(ch_hi_ok, 1)

            def mix_high(l, o):
                h = ORDER[o]
                act.wait_ge(product_ok, HEADS * l + (o + 1))
                nc.scalar.activation(middle(mix_hi, h), product[o % 4][:, 0:head_taps(h) * HD], ACT.Copy).then_inc(mix_hi_ok, 1)

            def evacuate(s, o):
                act.wait_ge(head_done, HEADS * s + (o + 1) + FREE)
                act.wait_ge(back_done, CHUNKS * s + o // 2 + FREE)
                nc.scalar.activation(mixed[:, o % 2, :], mixed_ps[o % 2][:, 0:PAIR * P], ACT.Copy).then_inc(mixed_ok, 1)

            def stage(l, pair):
                s = 2 * l + pair
                for c in range(CHUNKS):
                    if c < CHUNKS - 1:
                        act.wait_ge(head_done, HEADS * s + 2 * c + FREE)
                        high(s, c + 1)
                    if c == 6:
                        root(s + 1)
                    evacuate(s, 2 * c)
                    if c == CHUNKS - 1:
                        high(s + 1, 0)
                    evacuate(s, 2 * c + 1)
                    if pair == 1 and c >= 1:
                        with act.If(l < LAYERS - 1):
                            mix_high(l + 1, 2 * c - 2)
                            mix_high(l + 1, 2 * c - 1)
                if pair == 1:
                    with act.If(l < LAYERS - 1):
                        mix_high(l + 1, HEADS - 2)
                        mix_high(l + 1, HEADS - 1)

            root(0)
            high(0, 0)
            for o in range(HEADS):
                mix_high(0, o)
            act.sem_inc(mixed_ok, 2)
            layers(act, stage)

        @block.vector
        def _(dve):
            def stats(s, pair, b):
                for q in range(QUARTERS):
                    nc.vector.bn_stats(bn[:, b, q, :], tokens[:, pair * PT + b * QUARTERS + q, :]).then_inc(norm_step, 1)

            def aggregate(s):
                wait_apart(dve, norm_step, NORM_STEPS * s + 8, passed)
                for b in range(PAIR):
                    nc.vector.bn_aggr(mv[:, b, :], bn[:, b, :, :].rearrange("p q s -> p (q s)")).then_inc(norm_step, 1)

            def deviate(s):
                dve.wait_ge(stat_done, 2 * s + 1)
                nc.vector.tensor_copy(gmv[:, :, :].rearrange("p b s -> p (b s)"), stat_ps[:, 0:4]).then_inc(norm_step, 1)
                dve.wait_ge(norm_step, NORM_STEPS * s + 11)
                nc.vector.tensor_tensor(dev[:, :], mv[:, :, 0], gmv[:, :, 0], ALU.subtract).then_inc(norm_step, 1)
                dve.wait_ge(norm_step, NORM_STEPS * s + 12)
                nc.vector.tensor_tensor(dev2[:, :], dev[:, :], dev[:, :], ALU.mult).then_inc(norm_step, 1)

            def variance(s):
                dve.wait_ge(stat_done, 2 * s + 2)
                nc.vector.scalar_tensor_tensor(var[:, :], stat2_ps[:, 0:2], EPS, gmv[:, :, 1], ALU.add, ALU.add).then_inc(norm_step, 1)

            def normalise(s, pair):
                dve.wait_ge(root_ok, s + 1)
                nc.vector.reciprocal(rstd[:, :], std[:, :]).then_inc(norm_step, 1)
                dve.wait_ge(norm_step, NORM_STEPS * s + 15)
                dve.wait_ge(chT_done, CHUNKS * s)
                for b in range(PAIR):
                    t0 = b * QUARTERS
                    for at, n in ((0, D), (D, XW - D)):
                        nc.vector.tensor_scalar(norm[:, t0:t0 + QUARTERS, at:at + n],
                                                tokens[:, pair * PT + t0:pair * PT + t0 + QUARTERS, 0:n],
                                                gmv[:, b, 0:1], rstd[:, b:b + 1], ALU.subtract, ALU.mult).then_inc(norm_step, 1)

            def low(s, c):
                dve.wait_ge(ch_hi_ok, CHUNKS * s + (c + 1))
                nc.vector.tensor_tensor(ch_lo[c % 2][:, :, :, LEAD:].rearrange("p b q n -> p (b q) n"), chT_ps[:, :, :],
                                        ch_hi[c % 2][:, :, :, LEAD:].rearrange("p b q n -> p (b q) n").bitcast(f32),
                                        ALU.subtract).then_inc(ch_ok, 1)

            def add_back(s, pair, c):
                dve.wait_ge(back_done, CHUNKS * s + (c + 1) + FREE)
                for j, h in enumerate(CHUNK_HEADS[c]):
                    t = tokens[:, pair * PT:(pair + 1) * PT, h * HD:(h + 1) * HD]
                    ins = nc.vector.tensor_tensor(t, t, back_ps[:, j, :, :].rearrange("p b (q d) -> p (b q) d", d=HD), ALU.add)
                ins.then_inc(summed, 1)

            def mix_product(l, o):
                h = ORDER[o]
                k = head_taps(h)
                row0 = head_place(h)[1]
                if isinstance(l, int):
                    if o >= 4:
                        dve.wait_ge(mix_ok, HEADS * l + o - 3)
                else:
                    dve.wait_ge(mix_ok, HEADS * l + (o - 3))
                lt = slice(l, l + 1) if isinstance(l, int) else bass.ds(l, 1)
                a = taps_sb[:, lt, h, 0:k].rearrange("p o k -> p (o k)")[:, :, None].to_broadcast([P, k, HD])
                b = mix_sb[:, lt, row0 // 32, :].to_broadcast([P, k, HD])
                nc.vector.tensor_tensor(product[o % 4][:, 0:k * HD].rearrange("p (k d) -> p k d", d=HD), a, b,
                                        ALU.mult).then_inc(product_ok, 1)

            def mix_low(l, o):
                h = ORDER[o]
                dve.wait_ge(mix_hi_ok, HEADS * l + (o + 1))
                nc.vector.tensor_tensor(middle(mix_lo, h), product[o % 4][:, 0:head_taps(h) * HD],
                                        middle(mix_hi, h).bitcast(f32), ALU.subtract).then_inc(mix_ok, 1)

            def stage(l, pair):
                s = 2 * l + pair
                for c in range(CHUNKS):
                    if c == 6:
                        variance(s + 1)
                    if c < CHUNKS - 1:
                        low(s, c + 1)
                    else:
                        low(s + 1, 0)
                    if c == 6:
                        normalise(s + 1, 1 - pair)
                    if c:
                        add_back(s, pair, c - 1)
                    if c < 2:
                        dve.wait_ge(summed, CHUNKS * s + FREE)
                        stats(s + 1, 1 - pair, c)
                    if c == 2:
                        aggregate(s + 1)
                    if c == 4:
                        deviate(s + 1)
                    if pair == 1 and c >= 1:
                        with dve.If(l < LAYERS - 1):
                            mix_product(l + 1, 2 * c - 2)
                            mix_product(l + 1, 2 * c - 1)
                            if c >= 2:
                                mix_low(l + 1, 2 * c - 4)
                                mix_low(l + 1, 2 * c - 3)
                add_back(s, pair, CHUNKS - 1)
                if pair == 1:
                    with dve.If(l < LAYERS - 1):
                        mix_product(l + 1, HEADS - 2)
                        mix_product(l + 1, HEADS - 1)
                        for o in range(HEADS - 4, HEADS):
                            mix_low(l + 1, o)

            dve.sem_inc(summed, FREE)
            dve.wait_ge(tokens_in[0], 16 * PAIR)
            for b in range(PAIR):
                stats(0, 0, b)
            aggregate(0)
            deviate(0)
            variance(0)
            normalise(0, 0)
            dve.wait_ge(taps_in, 32)
            low(0, 0)
            for o in range(HEADS):
                mix_product(0, o)
                if o >= 2:
                    mix_low(0, o - 2)
            mix_low(0, HEADS - 2)
            mix_low(0, HEADS - 1)
            dve.wait_ge(tokens_in[1], 16 * PAIR)
            layers(dve, stage)

        @block.tensor
        def _(pe):
            def mean_over_groups(s, second):
                pe.wait_ge(norm_step, NORM_STEPS * s + (13 if second else 10))
                if second:
                    ins = nc.tensor.matmul(stat2_ps[:, 0:PAIR], group_mean[:, :], dev2[:, :], start=True, stop=True)
                else:
                    ins = nc.tensor.matmul(stat_ps[:, 0:2 * PAIR], group_mean[:, :], mv[:, :, :].rearrange("p b s -> p (b s)"), start=True, stop=True)
                ins.then_inc(stat_done, 1)

            def transpose_chunk(c):
                at = c * P if c < D // P else (c - D // P) * P + 64
                for i in range(PT):
                    last = nc.tensor.transpose(chT_ps[:, i, :], norm[:, i, at:at + P], ident[:, :])
                last.then_inc(chT_done, 1)

            def head(l, s, o):
                h = ORDER[o]
                k, c = head_taps(h), o // 2
                pe.wait_ge(mix_ok, HEADS * l + (o + 1))
                pe.wait_ge(mixed_ok, HEADS * s + (o + 1))
                res = mixed_ps[o % 2][:, 0:PAIR * P].rearrange("p (b n) -> p b n", b=PAIR)
                shifts = range(-(k - 1), PHASES)
                for r in shifts:
                    a, q = r // PHASES, r % PHASES
                    at = MIX_AT[h] + (PHASES - 1 - r) * HD
                    for w, x in ((mix_hi, ch_hi), (mix_hi, ch_lo), (mix_lo, ch_hi)):
                        last = nc.tensor.matmul(res, w[:, at:at + P], x[c % 2][:, :, q, LEAD + a:LEAD + a + P],
                                                start=(r == shifts[0] and w is mix_hi and x is ch_hi),
                                                stop=(r == shifts[-1] and w is mix_lo))
                last.then_inc(head_done, 1)

            def back(s, c):
                pe.wait_ge(summed, CHUNKS * s + c + FREE)
                pe.wait_ge(mixed_ok, HEADS * s + (2 * c + 4))
                for j in range(2):
                    for b in range(PAIR):
                        last = nc.tensor.transpose(back_ps[:, j, b, :], mixed[:, j, b * P:(b + 1) * P], ident[:, :])
                last.then_inc(back_done, 1)

            def stage(l, pair):
                s = 2 * l + pair
                for c in range(CHUNKS):
                    pe.wait_ge(ch_ok, CHUNKS * s + (c + 1))
                    if c < CHUNKS - 1:
                        transpose_chunk(c + 1)
                    head(l, s, 2 * c)
                    if c == 3:
                        mean_over_groups(s + 1, False)
                    if c == 5:
                        mean_over_groups(s + 1, True)
                    if c == CHUNKS - 1:
                        pe.wait_ge(norm_step, NORM_STEPS * (s + 2))
                        transpose_chunk(0)
                    head(l, s, 2 * c + 1)
                    if c:
                        back(s, c - 1)
                back(s, CHUNKS - 1)

            pe.sem_inc(head_done, FREE)
            pe.sem_inc(back_done, FREE)
            mean_over_groups(0, False)
            mean_over_groups(0, True)
            pe.wait_ge(norm_step, NORM_STEPS)
            transpose_chunk(0)
            pe.wait_ge(zeroed, 4 + 4 * HEADS)
            layers(pe, stage)


_OUT = (BATCH, SEQ, 16, 32)


def kernel(**inputs):
    import numpy as np
    import concourse.bacc as bacc
    from concourse.bass_utils import run_bass_kernel_spmd

    a = {k: np.asarray(v) for k, v in inputs.items()}
    w1, w3, w2 = a["L0_conv_w1"], a["L0_conv_w3"], a["L0_conv_w2"]
    w13T = np.stack([w.transpose(0, 2, 1).reshape(E, KD, P, F) for w in (w1, w3)], axis=3)
    w2T = w2.transpose(0, 2, 1).reshape(E, KF, P, D).transpose(0, 2, 1, 3)
    gate_wT = a["L0_conv_gate_w"].T.reshape(KD, P, E).transpose(1, 0, 2)
    taps = np.zeros((P, LAYERS, HEADS, TAPS), np.float32)
    mixT = np.zeros((P, LAYERS, 2, HD), np.float32)
    for l in range(LAYERS):
        filters = [a[f"L{l + 1}_conv_w{k}"] for k in SCALES]
        for v in range(2):
            mixT[32 * v:32 * v + HEAD_IN, l, v, :] = a[f"L{l + 1}_conv_w_mix"].T
        for h in range(HEADS):
            row0 = head_place(h)[1]
            for m in range(HEAD_IN):
                scale, channel = divmod(HEAD_IN * h + m, D)
                taps[row0 + m, l, h, 0:SCALES[scale]] = filters[scale][channel, 0, ::-1]
    arrays = {"x": a["x"], "gate_wT": gate_wT, "w13T": w13T, "w2T": w2T, "taps": taps, "mixT": mixT}
    arrays = {f"in_{k}": np.ascontiguousarray(v) for k, v in arrays.items()}

    nc = bacc.Bacc("TRN2", target_bir_lowering=False, num_devices=1)
    args = [nc.dram_tensor(k, v.shape, mybir.dt.from_np(v.dtype), kind="ExternalInput").ap() for k, v in arrays.items()]
    out = nc.dram_tensor("out", _OUT, mybir.dt.float32, kind="ExternalOutput").ap()
    build(nc, *args, out)
    return run_bass_kernel_spmd(nc, [arrays], core_ids=[0]).results[0]["out"]
```

```python
import concourse.bass as bass
from concourse import mybir
from contextlib import ExitStack

P = 128
BATCH, SEQ, D, F, E = 4, 512, 512, 1024, 8
QUARTERS = SEQ // P
TILES = BATCH * QUARTERS
TOKENS = BATCH * SEQ
TOP_K = 2
KD = D // P
KF = F // P
GROUP = SEQ // 32
GROUP_LANES = GROUP // QUARTERS
EPS = 1e-5
MAX_BLOCKS = (TOP_K * TOKENS + E * (P - 1)) // P
META = 4
ROW = D + META
LOW = -3.0e38
FREE = 1

LAYERS, HEADS, HD = 3, 16, 32
SCALES = (3, 7, 15)
HEAD_IN = len(SCALES) * HD
PHASES = QUARTERS
PAIR = 2
PT = PAIR * QUARTERS
LEAD = 4
CHUNKS = 8
XW = D + 64


def head_place(h):
    start = HEAD_IN * h % D
    if start % P <= P - HEAD_IN:
        return start // P, start % P
    return D // P + (start - 64) // P, (start - 64) % P


def head_taps(h):
    return SCALES[min((HEAD_IN * h + HEAD_IN - 1) // D, 2)]


CHUNK_HEADS = [[h for h in range(HEADS) if head_place(h)[0] == c] for c in range(CHUNKS)]
ORDER = [h for hs in CHUNK_HEADS for h in hs]
MIX_AT, _at = {}, 0
for _h in range(HEADS):
    MIX_AT[_h] = _at
    _at += (head_taps(_h) + 2 * (PHASES - 1)) * HD
MIX_COLS = _at
TAPS = max(SCALES)
MIX_MAX = TAPS * HD
EARLY = 6


def build(nc, x, gate_wT, w13T, w2T, taps, mixT, out):
    f32, f32r, i32, u32 = mybir.dt.float32, mybir.dt.float32r, mybir.dt.int32, mybir.dt.uint32
    ALU, ACT, AX = mybir.AluOpType, mybir.ActivationFunctionType, mybir.AxisListType

    slots_x = nc.dram_tensor("slots_x", [(MAX_BLOCKS + 2) * P, ROW], f32).ap()
    acc = nc.dram_tensor("acc", [TOKENS + P, D], f32).ap()
    with ExitStack() as ctx:
        def sb(name, shape):
            return ctx.enter_context(nc.sbuf_tensor(name, shape, f32))

        ident = sb("ident", [P, P])
        group_mean = sb("group_mean", [P, P])
        taps_sb = sb("taps_sb", [P, LAYERS + 1, HEADS, TAPS])
        mix_sb = sb("mix_sb", [P, LAYERS + 1, 2, HD])
        taps_in = ctx.enter_context(nc.semaphore("taps_in"))
        experts_part(nc, x, gate_wT, w13T, w2T, slots_x, acc, ident, group_mean, taps, mixT, taps_sb, mix_sb, taps_in)
        conv_part(nc, acc, out, ident, group_mean, taps_sb, mix_sb, taps_in)


def wait_apart(eng, semaphore, value, counter):
    eng.wait_ge(semaphore, value)
    eng.sem_inc(counter, 1)


def experts_part(nc, x, gate_wT, w13T, w2T, slots_x, acc, ident, group_mean, taps, mixT, taps_sb, mix_sb, taps_in):
    f32, f32r, i32, u32 = mybir.dt.float32, mybir.dt.float32r, mybir.dt.int32, mybir.dt.uint32
    ALU, ACT, AX = mybir.AluOpType, mybir.ActivationFunctionType, mybir.AxisListType
    x_rows = x.rearrange("b (p q) h w -> b p q (h w)", q=QUARTERS)

    with ExitStack() as ctx:
        def sb(name, shape, dt=f32):
            return ctx.enter_context(nc.sbuf_tensor(name, shape, dt))

        def ps(name, shape):
            return ctx.enter_context(nc.psum_tensor(name, shape, f32))

        def sem(name):
            return ctx.enter_context(nc.semaphore(name))

        w13_raw = sb("w13_raw", [P, KD, 2, F])
        w13_hi = sb("w13_hi", [P, KD, 2, F], f32r)
        w13_lo = sb("w13_lo", [P, KD, 2, F], f32r)
        w2_raw = sb("w2_raw", [P, KF, D])
        w2_hi = sb("w2_hi", [P, KF, D], f32r)
        w2_lo = sb("w2_lo", [P, KF, D], f32r)
        rows = sb("rows", [P, TILES, ROW])
        block_row = sb("block_row", [P, D])
        xT_hi = sb("xT_hi", [P, KD, P], f32r)
        xT_lo = sb("xT_lo", [P, KD, P], f32r)
        silu = sb("silu", [P, F])
        hidden = sb("hidden", [P, F])
        hT_hi = sb("hT_hi", [P, KF, P], f32r)
        hT_lo = sb("hT_lo", [P, KF, P], f32r)
        y_row = sb("y_row", [P, ROW])
        meta = sb("meta", [P, META])
        my_slot = sb("my_slot", [P, 1])
        weight = sb("weight", [P, 1])
        gate_sb = sb("gate_sb", [P, KD, E])
        early_w2 = w2_raw[:, :, :].rearrange("p k n -> p (k n)")
        gate_xT = early_w2.rearrange("p (s k n) -> p s k n", s=2, k=KD)
        place = early_w2[:, 0:TILES * P].rearrange("p (i s) -> p i s", s=P)
        pad_row = y_row[:, :]
        bn = sb("bn", [P, BATCH, QUARTERS, 6])
        mv = sb("mv", [P, BATCH, 2])
        gmv = sb("gmv", [P, BATCH, 2])
        dev = sb("dev", [P, BATCH, 2])
        rstd = sb("rstd", [P, BATCH, 4])
        ids = sb("ids", [P, TILES], i32)
        pad_id = sb("pad_id", [P, 1], i32)
        rev = sb("rev", [P, E])
        thresholds = sb("thresholds", [P, TILES - 1])
        lg, eq, score, pick1, pick2, lg2, mask, slot = (
            hidden[:, n * P:(n + 1) * P].rearrange("p (i e) -> p i e", e=E) for n in range(8))
        logits_T = hidden[0:E, :].rearrange("e (s n) -> e s n", s=2)
        restart, totals, running = (
            silu[:, n * P:(n + 1) * P].rearrange("p (e i) -> p e i", i=TILES) for n in range(3))
        before, ones, slot_row = (silu[:, n * P:(n + 1) * P] for n in range(3, 6))
        best = silu[:, 6 * P:7 * P].rearrange("p (n i) -> p n i", n=8)
        over = silu[:, 7 * P:8 * P - E].rearrange("p (e n) -> p e n", e=E)
        nblocks = sb("nblocks", [P, 4, E])
        slot_id = sb("slot_id", [P, TOP_K, TILES], i32)
        table = sb("table", [1, 16], i32)

        xT_ps = ps("xT_ps", [P, 512])
        gate_ps = ps("gate_ps", [P, 2, 512])
        up_ps = ps("up_ps", [P, 2, 512])
        hT_ps = ps("hT_ps", [P, KF, P])
        y_ps = ps("y_ps", [P, 512])
        gate_banks = [gate_ps[:, n, :] for n in range(2)] + [
            hT_ps[:, n * 4:n * 4 + 4, :].rearrange("p k n -> p (k n)") for n in range(2)]

        x_in = [sem(f"x_in{b}") for b in range(BATCH)]
        gate_in = sem("gate_in")
        acc_ready = sem("acc_ready")
        consts = sem("consts")
        pool_step = sem("pool_step")
        d_step = sem("d_step")
        averaged = sem("averaged")
        stat_ps = sem("stat_ps")
        centred = sem("centred")
        rooted = sem("rooted")
        normed = sem("normed")
        gxT_ps = sem("gxT_ps")
        gxT_sb = sem("gxT_sb")
        gate_done = sem("gate_done")
        logits_T_ok = sem("logits_T_ok")
        logits = sem("logits")
        ranks = sem("ranks")
        mask_ready = sem("mask_ready")
        gap_ready = sem("gap_ready")
        exped = sem("exped")
        table_ready = sem("table_ready")
        pads_in = sem("pads_in")
        rows_ready = sem("rows_ready")
        place_ok = sem("place_ok")
        scattered = sem("scattered")
        w13_in = [sem(f"w13_in{k}") for k in range(KD)]
        w2_in = [sem(f"w2_in{k}") for k in range(2)]
        w13_hi_ok = sem("w13_hi_ok")
        w13_ok = sem("w13_ok")
        w2_hi_ok = sem("w2_hi_ok")
        w2_ok = sem("w2_ok")
        row_in = sem("row_in")
        xT_done = sem("xT_done")
        xT_hi_ok = sem("xT_hi_ok")
        xT_ok = sem("xT_ok")
        up_done = sem("up_done")
        silu_ok = sem("silu_ok")
        hidden_ok = sem("hidden_ok")
        hT_done = sem("hT_done")
        hT_hi_ok = sem("hT_hi_ok")
        hT_ok = sem("hT_ok")
        down_done = sem("down_done")
        y_ok = sem("y_ok")
        meta_in = sem("meta_in")
        weight_ok = sem("weight_ok")
        w_step = sem("w_step")
        added = sem("added")
        passed = sem("passed")

        block = ctx.enter_context(nc.Block(name="experts"))

        def load_w13(eng, e, k):
            eng.dma_start(w13_raw[:, k], w13T[bass.ds(e, 1), k].rearrange("o p t n -> (o p) t n"))\
               .then_inc(w13_in[k], 16)

        def load_w2(eng, e, half):
            k = slice(half * KF // 2, (half + 1) * KF // 2)
            eng.dma_start(w2_raw[:, k], w2T[bass.ds(e, 1), :, k].rearrange("o p t n -> (o p) t n"))\
               .then_inc(w2_in[half], 16)

        def last_block_of(eng, e):
            return eng.value_load(table[0:1, bass.ds(e, 1)], min_val=0, max_val=MAX_BLOCKS - 1)

        def all_blocks(eng, new_expert, body, after_first):
            def one_expert(e, first, last):
                if not isinstance(e, int):
                    new_expert(e, first)
                body(e, first, True)
                after_first(e, first)
                with eng.If(last > first):
                    with eng.Fori(first + 1, last + 1) as g:
                        body(e, g, False)
            one_expert(0, 0, last_block_of(eng, 0))
            with eng.Fori(1, E) as e:
                one_expert(e, last_block_of(eng, e - 1) + 1, last_block_of(eng, e))

        @block.sync
        def _(sp):
            for b in range(BATCH):
                sp.dma_start(rows[:, b * QUARTERS:(b + 1) * QUARTERS, 0:D], x_rows[b]).then_inc(x_in[b], 16)
            for k in range(KD):
                load_w13(sp, 0, k)
            sp.wait_ge(table_ready, 1)
            sp.wait_ge(consts, 2)
            lasts = [last_block_of(sp, e) for e in range(E)]
            for last in lasts + [lasts[-1] + 1]:
                sp.dma_start(slots_x[bass.ds(last * P, P), :], pad_row).then_inc(pads_in, 16)
            sp.wait_ge(xT_done, 1)
            for half in range(2):
                load_w2(sp, 0, half)
            sp.wait_ge(scattered, 16 * TOP_K * TILES)
            sp.dma_start(taps_sb[:, 0:LAYERS], taps).then_inc(taps_in, 16)
            sp.dma_start(mix_sb[:, 0:LAYERS], mixT).then_inc(taps_in, 16)
            with sp.Fori(1, E) as e:
                for k in range(KD):
                    sp.wait_ge(w13_ok, (e - 1) * KD + k + 1)
                    load_w13(sp, e, k)
                for half in range(2):
                    sp.wait_ge(w2_ok, (e - 1) * 2 + half + 1)
                    load_w2(sp, e, half)

        @block.gpsimd
        def _(pool):
            steps = [0]

            def step(ins):
                steps[0] += 1
                ins.then_inc(pool_step, 1)
                pool.wait_ge(pool_step, steps[0])

            step(nc.gpsimd.memset(ident[:, :], 0.0))
            step(nc.gpsimd.affine_select(out=ident[:, :], in_=ident[:, :], compare_op=ALU.not_equal, fill=1.0,
                                         base=0, pattern=[[-1, P]], channel_multiplier=1))
            step(nc.gpsimd.memset(group_mean[:, :], 1.0 / GROUP_LANES))
            blocks = group_mean[:, :].rearrange("p (a c) -> p a c", c=GROUP_LANES)
            step(nc.gpsimd.affine_select(out=blocks, in_=blocks, compare_op=ALU.is_ge, fill=0.0, base=0,
                                         pattern=[[-GROUP_LANES, P // GROUP_LANES], [0, GROUP_LANES]],
                                         channel_multiplier=1))
            step(nc.gpsimd.affine_select(out=blocks, in_=blocks, compare_op=ALU.is_ge, fill=0.0,
                                         base=GROUP_LANES - 1,
                                         pattern=[[GROUP_LANES, P // GROUP_LANES], [0, GROUP_LANES]],
                                         channel_multiplier=-1))
            nc.gpsimd.memset(ones, 1.0).then_inc(consts, 1)
            step(nc.gpsimd.memset(before, 1.0))
            step(nc.gpsimd.affine_select(out=before, in_=before, compare_op=ALU.is_ge, fill=0.0,
                                         base=-1, pattern=[[1, P]], channel_multiplier=-1))
            step(nc.gpsimd.memset(pad_row, 0.0))
            step(nc.gpsimd.memset(pad_row[:, D + 1:D + 2], -1.0))
            step(nc.gpsimd.iota(pad_id[:, :], pattern=[[0, 1]], base=TOKENS, channel_multiplier=1))
            step(nc.gpsimd.tensor_copy(pad_row[:, D:D + 1].bitcast(i32), pad_id[:, :]))
            step(nc.gpsimd.iota(ids[:, :].rearrange("p (b q) -> p b q", q=QUARTERS),
                                pattern=[[SEQ, BATCH], [1, QUARTERS]], base=0, channel_multiplier=QUARTERS))
            step(nc.gpsimd.iota(rev[:, :], pattern=[[-1, E]], base=E, channel_multiplier=0,
                                allow_small_or_imprecise_dtypes=True))
            step(nc.gpsimd.iota(thresholds[:, :], pattern=[[P, TILES - 1]], base=P, channel_multiplier=0,
                                allow_small_or_imprecise_dtypes=True))
            step(nc.gpsimd.iota(slot_row, pattern=[[1, P]], base=0, channel_multiplier=0,
                                allow_small_or_imprecise_dtypes=True))
            step(nc.gpsimd.iota(my_slot[:, :], pattern=[[0, 1]], base=0, channel_multiplier=1,
                                allow_small_or_imprecise_dtypes=True))
            step(nc.gpsimd.memset(restart[:, :, :], 1.0))
            nc.gpsimd.memset(restart[:, :, 0:1], 0.0).then_inc(consts, 1)
            pool.wait_ge(w13_in[KD - 1], 16)
            pool.dma_start(acc[0:TOKENS, :].rearrange("(p a) n -> p (a n)", p=P),
                           x.rearrange("b (p a) h w -> (b p) (a h w)", a=TOKENS // P)).then_inc(acc_ready, 16)
            pool.dma_start(acc[TOKENS:TOKENS + P, :], pad_row[:, 0:D]).then_inc(acc_ready, 16)

            pool.wait_ge(rows_ready, 1)
            pool.wait_ge(pads_in, 16 * (E + 1))
            for j in range(TOP_K):
                for i in range(TILES):
                    pool.indirect_dma_start(
                        out=slots_x[:, :], out_offset=bass.IndirectOffsetOnAxis(slot_id[:, j, i:i + 1].bitcast(u32), 0),
                        in_=rows[:, i, :], in_offset=None).then_inc(scattered, 16)
            pool.wait_ge(scattered, 16 * TOP_K * TILES)
            pool.wait_ge(acc_ready, 32)

            def add_block(g):
                wait_apart(pool, y_ok, g + 1 + FREE, passed)
                pool.indirect_dma_start(
                    out=acc[:, :], out_offset=bass.IndirectOffsetOnAxis(meta[:, 0:1].bitcast(u32), 0),
                    in_=y_row[:, 0:D], in_offset=None, compute_op=ALU.add).then_inc(added, 16)
                wait_apart(pool, added, 16 * (g + 1), passed)

            def weigh_block(g):
                pool.dma_start(meta[:, :], slots_x[bass.ds(g * P, P), D:ROW]).then_inc(meta_in, 16)
                wait_apart(pool, meta_in, 16 * (g + 1), passed)
                nc.gpsimd.tensor_scalar(weight[:, :], meta[:, 1:2], my_slot[:, :], meta[:, 3:4],
                                        ALU.is_equal, ALU.mult).then_inc(w_step, 1)
                wait_apart(pool, w_step, 2 * g + 1, passed)
                nc.gpsimd.tensor_scalar(my_slot[:, :], my_slot[:, :], float(P), None, ALU.add).then_inc(w_step, 1)
                nc.gpsimd.tensor_tensor(weight[:, :], weight[:, :], meta[:, 2:3], ALU.add).then_inc(weight_ok, 1)
                wait_apart(pool, w_step, 2 * g + 2, passed)
                wait_apart(pool, weight_ok, g + 1, passed)

            def body(e, g, first):
                pool.wait_ge(xT_done, g + 1)
                pool.dma_start(block_row[:, :], slots_x[bass.ds((g + 1) * P, P), 0:D]).then_inc(row_in, 16)
                if isinstance(g, int):
                    return
                with pool.If(g > 1):
                    add_block(g - 2)
                weigh_block(g - 1)

            all_blocks(pool, lambda e, g: None, body, lambda e, g: None)
            g = last_block_of(pool, E - 1)
            add_block(g - 1)
            weigh_block(g)
            add_block(g)
            pool.wait_ge(row_in, 16 * (g + 1))

        @block.scalar
        def _(act):
            act.sem_inc(y_ok, FREE)
            act.dma_start(gate_sb[:, :, :], gate_wT).then_inc(gate_in, 16)

            def root(b):
                act.wait_ge(rooted, 2 * b + 1)
                nc.scalar.activation(rstd[:, b, 1:2], rstd[:, b, 0:1], ACT.Sqrt).then_inc(rooted, 1)

            def copy_gate_xT(b):
                if b >= 2:
                    act.wait_ge(gate_done, b - 1)
                for k in range(KD):
                    act.wait_ge(gxT_ps, KD * b + k + 1)
                    nc.scalar.activation(gate_xT[:, b % 2, k, :], gate_banks[k], ACT.Copy).then_inc(gxT_sb, 1)

            def copy_logits_T(b):
                act.wait_ge(gate_done, b + 1)
                if b >= 2:
                    act.wait_ge(logits, b - 1)
                nc.scalar.activation(logits_T[:, b % 2, :], xT_ps[0:E, :], ACT.Copy).then_inc(logits_T_ok, 1)

            for b in range(BATCH):
                root(b)
                if b:
                    copy_logits_T(b - 1)
                copy_gate_xT(b)
            copy_logits_T(BATCH - 1)
            act.wait_ge(gap_ready, 1)
            nc.scalar.activation(best[:, 3, :], best[:, 2, :], ACT.Exp).then_inc(exped, 1)

            def split_w13(e, g0):
                for k in range(KD):
                    act.wait_ge(w13_in[k], 16 * (e + 1))
                    if not isinstance(e, int):
                        act.wait_ge(up_done, g0 * KD + (k + 1 - KD))
                    nc.scalar.activation(w13_hi[:, k], w13_raw[:, k], ACT.Copy).then_inc(w13_hi_ok, 1)

            def split_w2(e, g0):
                if not isinstance(e, int):
                    act.wait_ge(down_done, g0 + FREE)
                for half in range(2):
                    act.wait_ge(w2_in[half], 16 * (e + 1))
                    k = slice(half * KF // 2, (half + 1) * KF // 2)
                    nc.scalar.activation(w2_hi[:, k], w2_raw[:, k], ACT.Copy).then_inc(w2_hi_ok, 1)

            def xT_high(g):
                act.wait_ge(xT_done, g + 1)
                nc.scalar.activation(xT_hi[:, :, :].rearrange("p a n -> p (a n)"), xT_ps[:, :], ACT.Copy).then_inc(xT_hi_ok, 1)

            def hT_high(g):
                act.wait_ge(hT_done, g + 1)
                act.wait_ge(down_done, g + FREE)
                nc.scalar.activation(hT_hi[:, :, :], hT_ps[:, :, :], ACT.Copy).then_inc(hT_hi_ok, 1)

            def weigh_y(g):
                act.wait_ge(down_done, g + 1 + FREE)
                act.wait_ge(weight_ok, g + 1)
                nc.scalar.activation(y_row[:, 0:D], y_ps[:, :], ACT.Copy, scale=weight[:, :]).then_inc(y_ok, 1)

            def body(e, g, first):
                if not isinstance(g, int):
                    with act.If(g > 1):
                        weigh_y(g - 2)
                    hT_high(g - 1)
                act.wait_ge(up_done, KD * (g + 1))
                if not isinstance(g, int):
                    act.wait_ge(hidden_ok, g)
                nc.scalar.activation(silu[:, :].rearrange("p (a n) -> p a n", a=2), gate_ps[:, :, :], ACT.Silu).then_inc(silu_ok, 1)
                xT_high(g + 1)

            act.wait_ge(table_ready, 1)
            split_w13(0, 0)
            xT_high(0)
            all_blocks(act, split_w13, body, split_w2)
            g = last_block_of(act, E - 1)
            weigh_y(g - 1)
            hT_high(g)
            weigh_y(g)

        @block.vector
        def _(dve):
            steps = [0]

            def step(ins):
                steps[0] += 1
                ins.then_inc(d_step, 1)
                dve.wait_ge(d_step, steps[0])

            def flush():
                dve.wait_ge(d_step, steps[0])

            def count(ins):
                steps[0] += 1
                ins.then_inc(d_step, 1)

            def lane_statistics(b):
                dve.wait_ge(x_in[b], 16)
                for q in range(QUARTERS):
                    count(nc.vector.bn_stats(bn[:, b, q, :], rows[:, b * QUARTERS + q, 0:D]))
                flush()
                nc.vector.bn_aggr(mv[:, b, :], bn[:, b, :, :].rearrange("p q s -> p (q s)")).then_inc(averaged, 1)

            def deviation(b):
                dve.wait_ge(stat_ps, 2 * b + 1)
                step(nc.vector.tensor_copy(gmv[:, b, :], up_ps[:, 0, 2 * b:2 * b + 2]))
                step(nc.vector.tensor_scalar(dev[:, b, 0:1], mv[:, b, 0:1], gmv[:, b, 0:1], None, ALU.subtract))
                nc.vector.tensor_tensor(dev[:, b, 1:2], dev[:, b, 0:1], dev[:, b, 0:1], ALU.mult).then_inc(centred, 1)

            def variance(b):
                dve.wait_ge(stat_ps, 2 * b + 2)
                nc.vector.tensor_scalar(rstd[:, b, 0:1], up_ps[:, 1, b:b + 1], gmv[:, b, 1:2], EPS, ALU.add, ALU.add).then_inc(rooted, 1)

            def normalise(b):
                dve.wait_ge(rooted, 2 * b + 2)
                step(nc.vector.reciprocal(rstd[:, b, 2:3], rstd[:, b, 1:2]))
                r = rows[:, b * QUARTERS:(b + 1) * QUARTERS, 0:D]
                nc.vector.tensor_scalar(r, r, gmv[:, b, 0:1], rstd[:, b, 2:3], ALU.subtract, ALU.mult).then_inc(normed, 1)

            for b in range(BATCH):
                lane_statistics(b)
                if b:
                    variance(b - 1)
                deviation(b)
                if b:
                    normalise(b - 1)
            variance(BATCH - 1)
            normalise(BATCH - 1)

            bc = [P, TILES, E]
            dve.wait_ge(consts, 2)
            dve.wait_ge(logits, BATCH)
            step(nc.vector.tensor_copy(lg[:, :, :].rearrange("p i e -> p (i e)"), y_ps[:, 0:TILES * E]))

            def pick(source, top, which, onehot):
                step(nc.vector.tensor_reduce(best[:, top, :], source, axis=AX.X, op=ALU.max))
                step(nc.vector.tensor_tensor(eq[:, :, :], source, best[:, top, :, None].to_broadcast(bc), ALU.is_equal))
                step(nc.vector.tensor_tensor(score[:, :, :], eq[:, :, :], rev[:, None, :].to_broadcast(bc), ALU.mult))
                step(nc.vector.tensor_reduce(best[:, which, :], score[:, :, :], axis=AX.X, op=ALU.max))
                step(nc.vector.tensor_tensor(onehot, score[:, :, :], best[:, which, :, None].to_broadcast(bc), ALU.is_equal))

            pick(lg[:, :, :], 0, 6, pick1[:, :, :])
            step(nc.vector.scalar_tensor_tensor(lg2[:, :, :], pick1[:, :, :], LOW, lg[:, :, :], ALU.mult, ALU.add))
            pick(lg2[:, :, :], 1, 7, pick2[:, :, :])
            nc.vector.tensor_tensor(mask[:, :, :], pick1[:, :, :], pick2[:, :, :], ALU.add).then_inc(mask_ready, 1)
            nc.vector.tensor_tensor(best[:, 2, :], best[:, 1, :], best[:, 0, :], ALU.subtract).then_inc(gap_ready, 1)
            dve.wait_ge(ranks, 2)
            step(nc.vector.tensor_copy(totals[:, :, :], hT_ps[:, 4, :].rearrange("p (i e) -> p e i", e=E)))
            step(nc.vector.tensor_tensor_scan(running[:, :, :].rearrange("p e i -> p (e i)"),
                                              restart[:, :, :].rearrange("p e i -> p (e i)"),
                                              totals[:, :, :].rearrange("p e i -> p (e i)"), 0.0, ALU.mult, ALU.add))
            step(nc.vector.tensor_tensor(over[:, :, :], running[:, :, TILES - 1:TILES].to_broadcast([P, E, TILES - 1]),
                                         thresholds[:, None, :].to_broadcast([P, E, TILES - 1]), ALU.is_gt))
            step(nc.vector.tensor_reduce(nblocks[:, 0, :], over[:, :, :], axis=AX.X, op=ALU.add))
            step(nc.vector.tensor_scalar(nblocks[:, 0, :], nblocks[:, 0, :], 1.0, None, ALU.add))
            step(nc.vector.tensor_tensor_scan(nblocks[:, 1, :], ones[:, 0:E], nblocks[:, 0, :], 0.0, ALU.mult, ALU.add))
            step(nc.vector.tensor_tensor(nblocks[:, 2, :], nblocks[:, 1, :], nblocks[:, 0, :], ALU.subtract))
            nc.vector.tensor_scalar(table[0:1, 0:E], nblocks[0:1, 1, :], 1.0, None, ALU.subtract).then_inc(table_ready, 1)
            step(nc.vector.tensor_scalar(nblocks[:, 3, :], nblocks[:, 2, :], float(P), None, ALU.mult))
            step(nc.vector.tensor_tensor(running[:, :, :], running[:, :, :], totals[:, :, :], ALU.subtract))
            step(nc.vector.tensor_tensor(running[:, :, :], running[:, :, :], nblocks[:, 3, :, None].to_broadcast([P, E, TILES]), ALU.add))
            step(nc.vector.tensor_tensor(slot[:, :, :], hT_ps[:, 0, :].rearrange("p (i e) -> p i e", e=E),
                                         running[:, :, :].rearrange("p e i -> p i e"), ALU.add))
            for j, onehot in enumerate((pick1, pick2)):
                step(nc.vector.tensor_tensor(eq[:, :, :], slot[:, :, :], onehot[:, :, :], ALU.mult))
                step(nc.vector.tensor_reduce(best[:, 6 + j, :], eq[:, :, :], axis=AX.X, op=ALU.add))
                step(nc.vector.tensor_copy(slot_id[:, j, :], best[:, 6 + j, :]))
            dve.wait_ge(exped, 1)
            step(nc.vector.tensor_scalar(best[:, 4, :], best[:, 3, :], 1.0, None, ALU.add))
            step(nc.vector.reciprocal(best[:, 5, :], best[:, 4, :]))
            step(nc.vector.tensor_tensor(rows[:, :, D + 2], best[:, 3, :], best[:, 5, :], ALU.mult))
            count(nc.vector.tensor_tensor(rows[:, :, D + 3], best[:, 5, :], rows[:, :, D + 2], ALU.subtract))
            count(nc.vector.tensor_copy(rows[:, :, D + 1], best[:, 6, :]))
            count(nc.vector.tensor_copy(rows[:, :, D].bitcast(i32), ids[:, :]))
            flush()
            dve.sem_inc(rows_ready, 1)
            step(nc.vector.tensor_tensor(best[:, 4, :], best[:, 6, :], best[:, 7, :], ALU.min))
            nc.vector.tensor_tensor(place, slot_row[:, None, :].to_broadcast([P, TILES, P]),
                                    best[:, 4, :, None].to_broadcast([P, TILES, P]), ALU.is_equal).then_inc(place_ok, 1)

            def split_w13(e, g0):
                for k in range(KD):
                    dve.wait_ge(w13_hi_ok, KD * e + (k + 1))
                    nc.vector.tensor_tensor(w13_lo[:, k], w13_raw[:, k], w13_hi[:, k].bitcast(f32),
                                            ALU.subtract).then_inc(w13_ok, 1)

            def split_w2(e, g0):
                for half in range(2):
                    dve.wait_ge(w2_hi_ok, 2 * e + (half + 1))
                    k = slice(half * KF // 2, (half + 1) * KF // 2)
                    nc.vector.tensor_tensor(w2_lo[:, k], w2_raw[:, k], w2_hi[:, k].bitcast(f32),
                                            ALU.subtract).then_inc(w2_ok, 1)

            def xT_low(g):
                dve.wait_ge(xT_hi_ok, g + 1)
                nc.vector.tensor_tensor(xT_lo[:, :, :].rearrange("p a n -> p (a n)"), xT_ps[:, :],
                                        xT_hi[:, :, :].rearrange("p a n -> p (a n)").bitcast(f32), ALU.subtract).then_inc(xT_ok, 1)

            def hT_low(g):
                dve.wait_ge(hT_hi_ok, g + 1)
                nc.vector.tensor_tensor(hT_lo[:, :, :], hT_ps[:, :, :], hT_hi[:, :, :].bitcast(f32),
                                        ALU.subtract).then_inc(hT_ok, 1)

            def body(e, g, first):
                if not isinstance(g, int):
                    hT_low(g - 1)
                dve.wait_ge(silu_ok, g + 1)
                if not isinstance(g, int):
                    dve.wait_ge(hT_done, g)
                nc.vector.tensor_tensor(hidden[:, :].rearrange("p (a n) -> p a n", a=2),
                                        silu[:, :].rearrange("p (a n) -> p a n", a=2), up_ps[:, :, :],
                                        ALU.mult).then_inc(hidden_ok, 1)
                xT_low(g + 1)

            dve.wait_ge(table_ready, 1)
            split_w13(0, 0)
            xT_low(0)
            all_blocks(dve, split_w13, body, split_w2)
            hT_low(last_block_of(dve, E - 1))

        @block.tensor
        def _(pe):
            pe.sem_inc(down_done, FREE)
            pe.wait_ge(pool_step, 5)

            def group_means(b):
                pe.wait_ge(averaged, b + 1)
                nc.tensor.matmul(up_ps[:, 0, 2 * b:2 * b + 2], group_mean[:, :], mv[:, b, :], start=True, stop=True).then_inc(stat_ps, 1)

            def group_deviation(b):
                pe.wait_ge(centred, b + 1)
                nc.tensor.matmul(up_ps[:, 1, b:b + 1], group_mean[:, :], dev[:, b, 1:2], start=True, stop=True).then_inc(stat_ps, 1)

            def transpose_batch(b):
                pe.wait_ge(normed, b + 1)
                for k in range(KD):
                    if b:
                        pe.wait_ge(gxT_sb, KD * (b - 1) + k + 1)
                    for q in range(QUARTERS):
                        last = nc.tensor.transpose(gate_banks[k][:, q * P:(q + 1) * P],
                                                   rows[:, b * QUARTERS + q, k * P:(k + 1) * P], ident[:, :])
                    last.then_inc(gxT_ps, 1)

            def gate_product(b, chunks):
                if b and chunks[0] == 0:
                    pe.wait_ge(logits_T_ok, b)
                for k in chunks:
                    pe.wait_ge(gxT_sb, KD * b + k + 1)
                    last = nc.tensor.matmul(xT_ps[0:E, :], gate_sb[:, k, :], gate_xT[:, b % 2, k, :],
                                            start=(k == 0), stop=(k == KD - 1))
                if chunks[-1] == KD - 1:
                    last.then_inc(gate_done, 1)

            def transpose_logits(b):
                pe.wait_ge(logits_T_ok, b + 1)
                for q in range(QUARTERS):
                    i = b * QUARTERS + q
                    last = nc.tensor.transpose(y_ps[:, i * E:(i + 1) * E], logits_T[:, b % 2, q * P:(q + 1) * P], ident[0:E, 0:E])
                last.then_inc(logits, 1)

            group_means(0)
            group_deviation(0)
            group_means(1)
            group_deviation(1)
            pe.wait_ge(gate_in, 16)
            for b in range(BATCH):
                transpose_batch(b)
                if b:
                    transpose_logits(b - 1)
                gate_product(b, range(KD // 2))
                if b + 2 < BATCH:
                    group_means(b + 2)
                gate_product(b, range(KD // 2, KD))
                if b + 2 < BATCH:
                    group_deviation(b + 2)
            transpose_logits(BATCH - 1)
            pe.wait_ge(mask_ready, 1)
            pe.wait_ge(consts, 1)
            pe.wait_ge(pool_step, 7)
            nc.tensor.matmul(hT_ps[:, 0, :], before, mask[:, :, :].rearrange("p i e -> p (i e)"), start=True, stop=True).then_inc(ranks, 1)
            nc.tensor.matmul(hT_ps[:, 4, :], ones, mask[:, :, :].rearrange("p i e -> p (i e)"), start=True, stop=True).then_inc(ranks, 1)

            def gather_block_0():
                pe.wait_ge(place_ok, 1)
                for k in range(KD):
                    for i in range(TILES):
                        last = nc.tensor.matmul(xT_ps[:, k * P:(k + 1) * P], rows[:, i, k * P:(k + 1) * P], place[:, i, :],
                                                start=(i == 0), stop=(i == TILES - 1))
                last.then_inc(xT_done, 1)

            def next_rows(g):
                pe.wait_ge(row_in, 16 * (g + 1))
                for k in range(KD):
                    last = nc.tensor.transpose(xT_ps[:, k * P:(k + 1) * P], block_row[:, k * P:(k + 1) * P], ident[:, :])
                last.then_inc(xT_done, 1)

            def down(g, w2_count):
                pe.wait_ge(y_ok, g + FREE)
                pe.wait_ge(w2_ok, w2_count)
                pe.wait_ge(hT_ok, g + 1)
                for k in range(KF):
                    for a, b in ((hT_hi, w2_hi), (hT_hi, w2_lo), (hT_lo, w2_hi)):
                        last = nc.tensor.matmul(y_ps[:, :], a[:, k, :], b[:, k, :],
                                                start=(k == 0 and b is w2_hi and a is hT_hi),
                                                stop=(k == KF - 1 and a is hT_lo))
                last.then_inc(down_done, 1)

            def body(e, g, first):
                pe.wait_ge(xT_ok, g + 1)
                for k in range(KD):
                    pe.wait_ge(w13_ok, KD * e + (k + 1))
                    for a, b in ((xT_hi, w13_hi), (xT_hi, w13_lo), (xT_lo, w13_hi)):
                        for t, o in ((0, gate_ps), (1, up_ps)):
                            for n in range(2):
                                last = nc.tensor.matmul(o[:, n, :], a[:, k, :], b[:, k, t, n * 512:(n + 1) * 512],
                                                        start=(k == 0 and a is xT_hi and b is w13_hi),
                                                        stop=(k == KD - 1 and a is xT_lo))
                    last.then_inc(up_done, 1)
                next_rows(g)
                if not isinstance(g, int):
                    down(g - 1, 2 * e if first else 2 * e + 2)
                pe.wait_ge(hidden_ok, g + 1)
                for k in range(KF):
                    last = nc.tensor.transpose(hT_ps[:, k, :], hidden[:, k * P:(k + 1) * P], ident[:, :])
                last.then_inc(hT_done, 1)

            pe.wait_ge(table_ready, 1)
            gather_block_0()
            all_blocks(pe, lambda e, g: None, body, lambda e, g: None)
            down(last_block_of(pe, E - 1), 2 * E)



def conv_part(nc, acc, out, ident, group_mean, taps_sb, mix_sb, taps_in):
    f32, f32r = mybir.dt.float32, mybir.dt.float32r
    ALU, ACT = mybir.AluOpType, mybir.ActivationFunctionType
    acc_rows = acc[0:TOKENS, :].rearrange("(b p q) n -> b p q n", p=P, q=QUARTERS)
    out_rows = out.rearrange("b (p q) h w -> b p q (h w)", q=QUARTERS)
    STATS, CENTRED, ROOTED, FIRST_CHUNK, NORM_STEPS = 10, 13, 14, 17, 21

    with ExitStack() as ctx:
        def sb(name, shape, dt=f32):
            return ctx.enter_context(nc.sbuf_tensor(name, shape, dt))

        def ps(name, shape):
            return ctx.enter_context(nc.psum_tensor(name, shape, f32))

        def sem(name):
            return ctx.enter_context(nc.semaphore(name))

        tokens = sb("tokens", [P, TILES, D])
        norm = sb("norm", [P, PT, XW])
        ch_hi = [sb(f"ch_hi{i}", [P, PAIR, QUARTERS, LEAD + P], f32r) for i in range(2)]
        ch_lo = [sb(f"ch_lo{i}", [P, PAIR, QUARTERS, LEAD + P], f32r) for i in range(2)]
        mix_hi = sb("mix_hi", [P, MIX_COLS], f32r)
        mix_lo = sb("mix_lo", [P, MIX_COLS], f32r)
        product = [sb(f"product{i}", [P, MIX_MAX]) for i in range(4)]
        mixed = sb("mixed", [P, 2, PAIR * P])
        bn = sb("bn_c", [P, PAIR, QUARTERS, 6])
        mv = sb("mv_c", [P, PAIR, 2])
        gmv = sb("gmv_c", [P, PAIR, 2])
        dev = sb("dev_c", [P, PAIR])
        dev2 = sb("dev2_c", [P, PAIR])
        var = sb("var_c", [P, PAIR])
        std = sb("std_c", [P, PAIR])
        rstd = sb("rstd_c", [P, PAIR])

        chT_ps = ps("chT_ps", [P, PT, P])
        mixed_ps = [ps(f"mixed_ps{i}", [P, 512]) for i in range(2)]
        back_ps = ps("back_ps", [P, 2, PAIR, P])
        stat_ps = ps("stat_ps", [P, 512])
        stat2_ps = ps("stat2_ps", [P, 512])

        half_in = [sem(f"half_in{i}") for i in range(2 * PAIR)]
        rest_in = sem("rest_in")
        zeroed = sem("zeroed")
        norm_step = sem("norm_step")
        stat_done = sem("stat_done")
        root_ok = sem("root_ok")
        chT_done = sem("chT_done")
        ch_hi_ok = sem("ch_hi_ok")
        ch_ok = sem("ch_ok")
        head_done = sem("head_done")
        mixed_ok = sem("mixed_ok")
        back_done = sem("back_done")
        summed = sem("summed")
        product_ok = sem("product_ok")
        mix_hi_ok = sem("mix_hi_ok")
        mix_ok = sem("mix_ok")
        stored = sem("stored")
        passed = sem("passed_c")
        block = ctx.enter_context(nc.Block(name="convolutions"))

        def middle(t, h):
            at = MIX_AT[h] + (PHASES - 1) * HD
            return t[:, at:at + head_taps(h) * HD]

        @block.sync
        def _(sp):
            for n in range(2 * PAIR):
                b, q = n // 2, n % 2 * 2
                sp.dma_start(tokens[:, 2 * n:2 * n + 2, :], acc_rows[b, :, q:q + 2]).then_inc(half_in[n], 16)
            for b in range(PAIR, BATCH):
                sp.dma_start(tokens[:, b * QUARTERS:(b + 1) * QUARTERS, :], acc_rows[b]).then_inc(rest_in, 16)
            for pair in range(2):
                sp.wait_ge(summed, CHUNKS * (2 * (LAYERS - 1) + pair + 1) + FREE)
                for b in range(pair * PAIR, (pair + 1) * PAIR):
                    sp.dma_start(out_rows[b], tokens[:, b * QUARTERS:(b + 1) * QUARTERS, :]).then_inc(stored, 16)
            sp.wait_ge(stored, 16 * BATCH)

        @block.gpsimd
        def _(pool):
            for i in range(2):
                nc.gpsimd.memset(ch_hi[i][:, :, :, 0:LEAD].bitcast(f32), 0.0).then_inc(zeroed, 1)
                nc.gpsimd.memset(ch_lo[i][:, :, :, 0:LEAD].bitcast(f32), 0.0).then_inc(zeroed, 1)
            for h in ORDER:
                for t in (mix_hi, mix_lo):
                    k = head_taps(h)
                    for at in (MIX_AT[h], MIX_AT[h] + (PHASES - 1 + k) * HD):
                        nc.gpsimd.memset(t[:, at:at + (PHASES - 1) * HD].bitcast(f32), 0.0).then_inc(zeroed, 1)

        def layers(eng, stage):
            with eng.Fori(0, LAYERS) as l:
                for pair in range(2):
                    stage(l, pair)

        @block.scalar
        def _(act):
            def root(s):
                act.wait_ge(norm_step, NORM_STEPS * s + ROOTED)
                nc.scalar.activation(std[:, :], var[:, :], ACT.Sqrt).then_inc(root_ok, 1)

            def high(s, c):
                act.wait_ge(chT_done, CHUNKS * s + (c + 1))
                nc.scalar.activation(ch_hi[c % 2][:, :, :, LEAD:].rearrange("p b q n -> p (b q) n"),
                                     chT_ps[:, :, :], ACT.Copy).then_inc(ch_hi_ok, 1)

            def mix_high(l, o):
                h = ORDER[o]
                act.wait_ge(product_ok, HEADS * l + (o + 1))
                nc.scalar.activation(middle(mix_hi, h), product[o % 4][:, 0:head_taps(h) * HD], ACT.Copy).then_inc(mix_hi_ok, 1)

            def evacuate(s, o):
                act.wait_ge(head_done, HEADS * s + (o + 1) + FREE)
                act.wait_ge(back_done, CHUNKS * s + o // 2 + FREE)
                nc.scalar.activation(mixed[:, o % 2, :], mixed_ps[o % 2][:, 0:PAIR * P], ACT.Copy).then_inc(mixed_ok, 1)

            def stage(l, pair):
                s = 2 * l + pair
                for c in range(CHUNKS):
                    if c < CHUNKS - 1:
                        act.wait_ge(head_done, HEADS * s + 2 * c + FREE)
                        high(s, c + 1)
                    if c == 6:
                        root(s + 1)
                    evacuate(s, 2 * c)
                    if c == CHUNKS - 1:
                        high(s + 1, 0)
                    evacuate(s, 2 * c + 1)
                    if pair == 1 and c >= 1:
                        with act.If(l < LAYERS - 1):
                            mix_high(l + 1, 2 * c - 2)
                            mix_high(l + 1, 2 * c - 1)
                if pair == 1:
                    with act.If(l < LAYERS - 1):
                        mix_high(l + 1, HEADS - 2)
                        mix_high(l + 1, HEADS - 1)

            for o in range(EARLY):
                mix_high(0, o)
            root(0)
            high(0, 0)
            for o in range(EARLY, HEADS):
                mix_high(0, o)
            act.sem_inc(mixed_ok, 2)
            layers(act, stage)

        @block.vector
        def _(dve):
            def stats(s, pair, b):
                for q in range(QUARTERS):
                    if s is None and q % 2 == 0:
                        dve.wait_ge(half_in[2 * b + q // 2], 16)
                    nc.vector.bn_stats(bn[:, b, q, :], tokens[:, pair * PT + b * QUARTERS + q, :]).then_inc(norm_step, 1)

            def aggregate(s):
                wait_apart(dve, norm_step, NORM_STEPS * s + 8, passed)
                for b in range(PAIR):
                    nc.vector.bn_aggr(mv[:, b, :], bn[:, b, :, :].rearrange("p q s -> p (q s)")).then_inc(norm_step, 1)

            def deviate(s):
                dve.wait_ge(stat_done, 2 * s + 1)
                nc.vector.tensor_copy(gmv[:, :, :].rearrange("p b s -> p (b s)"), stat_ps[:, 0:4]).then_inc(norm_step, 1)
                dve.wait_ge(norm_step, NORM_STEPS * s + 11)
                nc.vector.tensor_tensor(dev[:, :], mv[:, :, 0], gmv[:, :, 0], ALU.subtract).then_inc(norm_step, 1)
                dve.wait_ge(norm_step, NORM_STEPS * s + 12)
                nc.vector.tensor_tensor(dev2[:, :], dev[:, :], dev[:, :], ALU.mult).then_inc(norm_step, 1)

            def variance(s):
                dve.wait_ge(stat_done, 2 * s + 2)
                nc.vector.scalar_tensor_tensor(var[:, :], stat2_ps[:, 0:2], EPS, gmv[:, :, 1], ALU.add, ALU.add).then_inc(norm_step, 1)

            def normalise(s, pair):
                dve.wait_ge(root_ok, s + 1)
                nc.vector.reciprocal(rstd[:, :], std[:, :]).then_inc(norm_step, 1)
                dve.wait_ge(norm_step, NORM_STEPS * s + 15)
                dve.wait_ge(chT_done, CHUNKS * s)
                for at, n in ((0, P), (P, D - P), (D, XW - D)):
                    for b in range(PAIR):
                        t0 = b * QUARTERS
                        source = at % D
                        nc.vector.tensor_scalar(norm[:, t0:t0 + QUARTERS, at:at + n],
                                                tokens[:, pair * PT + t0:pair * PT + t0 + QUARTERS, source:source + n],
                                                gmv[:, b, 0:1], rstd[:, b:b + 1], ALU.subtract, ALU.mult).then_inc(norm_step, 1)

            def low(s, c):
                dve.wait_ge(ch_hi_ok, CHUNKS * s + (c + 1))
                nc.vector.tensor_tensor(ch_lo[c % 2][:, :, :, LEAD:].rearrange("p b q n -> p (b q) n"), chT_ps[:, :, :],
                                        ch_hi[c % 2][:, :, :, LEAD:].rearrange("p b q n -> p (b q) n").bitcast(f32),
                                        ALU.subtract).then_inc(ch_ok, 1)

            def add_back(s, pair, c):
                dve.wait_ge(back_done, CHUNKS * s + (c + 1) + FREE)
                for j, h in enumerate(CHUNK_HEADS[c]):
                    t = tokens[:, pair * PT:(pair + 1) * PT, h * HD:(h + 1) * HD]
                    ins = nc.vector.tensor_tensor(t, t, back_ps[:, j, :, :].rearrange("p b (q d) -> p (b q) d", d=HD), ALU.add)
                ins.then_inc(summed, 1)

            def mix_product(l, o):
                h = ORDER[o]
                k = head_taps(h)
                row0 = head_place(h)[1]
                if isinstance(l, int):
                    if o >= 4:
                        dve.wait_ge(mix_ok, HEADS * l + o - 3)
                else:
                    dve.wait_ge(mix_ok, HEADS * l + (o - 3))
                lt = slice(l, l + 1) if isinstance(l, int) else bass.ds(l, 1)
                a = taps_sb[:, lt, h, 0:k].rearrange("p o k -> p (o k)")[:, :, None].to_broadcast([P, k, HD])
                b = mix_sb[:, lt, row0 // 32, :].to_broadcast([P, k, HD])
                nc.vector.tensor_tensor(product[o % 4][:, 0:k * HD].rearrange("p (k d) -> p k d", d=HD), a, b,
                                        ALU.mult).then_inc(product_ok, 1)

            def mix_low(l, o):
                h = ORDER[o]
                dve.wait_ge(mix_hi_ok, HEADS * l + (o + 1))
                nc.vector.tensor_tensor(middle(mix_lo, h), product[o % 4][:, 0:head_taps(h) * HD],
                                        middle(mix_hi, h).bitcast(f32), ALU.subtract).then_inc(mix_ok, 1)

            def stage(l, pair):
                s = 2 * l + pair
                for c in range(CHUNKS):
                    if c == 6:
                        variance(s + 1)
                    if c < CHUNKS - 1:
                        low(s, c + 1)
                    else:
                        low(s + 1, 0)
                    if c == 6:
                        normalise(s + 1, 1 - pair)
                    if c:
                        add_back(s, pair, c - 1)
                    if c < 2:
                        dve.wait_ge(summed, CHUNKS * s + FREE)
                        stats(s + 1, 1 - pair, c)
                    if c == 2:
                        aggregate(s + 1)
                    if c == 4:
                        deviate(s + 1)
                    if pair == 1 and c >= 1:
                        with dve.If(l < LAYERS - 1):
                            mix_product(l + 1, 2 * c - 2)
                            mix_product(l + 1, 2 * c - 1)
                            if c >= 2:
                                mix_low(l + 1, 2 * c - 4)
                                mix_low(l + 1, 2 * c - 3)
                add_back(s, pair, CHUNKS - 1)
                if pair == 1:
                    with dve.If(l < LAYERS - 1):
                        mix_product(l + 1, HEADS - 2)
                        mix_product(l + 1, HEADS - 1)
                        for o in range(HEADS - 4, HEADS):
                            mix_low(l + 1, o)

            dve.sem_inc(summed, FREE)
            dve.wait_ge(taps_in, 32)
            for o in range(EARLY):
                mix_product(0, o)
                if o >= 3:
                    mix_low(0, o - 3)
            for b in range(PAIR):
                stats(None, 0, b)
            aggregate(0)
            mix_low(0, EARLY - 3)
            deviate(0)
            mix_low(0, EARLY - 2)
            variance(0)
            mix_low(0, EARLY - 1)
            normalise(0, 0)
            low(0, 0)
            for o in range(EARLY, HEADS):
                mix_product(0, o)
                if o >= EARLY + 2:
                    mix_low(0, o - 2)
            mix_low(0, HEADS - 2)
            mix_low(0, HEADS - 1)
            dve.wait_ge(rest_in, 16 * PAIR)
            layers(dve, stage)

        @block.tensor
        def _(pe):
            def mean_over_groups(s, second):
                pe.wait_ge(norm_step, NORM_STEPS * s + (CENTRED if second else STATS))
                if second:
                    ins = nc.tensor.matmul(stat2_ps[:, 0:PAIR], group_mean[:, :], dev2[:, :], start=True, stop=True)
                else:
                    ins = nc.tensor.matmul(stat_ps[:, 0:2 * PAIR], group_mean[:, :], mv[:, :, :].rearrange("p b s -> p (b s)"), start=True, stop=True)
                ins.then_inc(stat_done, 1)

            def transpose_chunk(c):
                at = c * P if c < D // P else (c - D // P) * P + 64
                for i in range(PT):
                    last = nc.tensor.transpose(chT_ps[:, i, :], norm[:, i, at:at + P], ident[:, :])
                last.then_inc(chT_done, 1)

            def head(l, s, o):
                h = ORDER[o]
                k, c = head_taps(h), o // 2
                pe.wait_ge(mix_ok, HEADS * l + (o + 1))
                pe.wait_ge(mixed_ok, HEADS * s + (o + 1))
                res = mixed_ps[o % 2][:, 0:PAIR * P].rearrange("p (b n) -> p b n", b=PAIR)
                shifts = range(-(k - 1), PHASES)
                for r in shifts:
                    a, q = r // PHASES, r % PHASES
                    at = MIX_AT[h] + (PHASES - 1 - r) * HD
                    for w, x in ((mix_hi, ch_hi), (mix_hi, ch_lo), (mix_lo, ch_hi)):
                        last = nc.tensor.matmul(res, w[:, at:at + P], x[c % 2][:, :, q, LEAD + a:LEAD + a + P],
                                                start=(r == shifts[0] and w is mix_hi and x is ch_hi),
                                                stop=(r == shifts[-1] and w is mix_lo))
                last.then_inc(head_done, 1)

            def back(s, c):
                pe.wait_ge(summed, CHUNKS * s + c + FREE)
                pe.wait_ge(mixed_ok, HEADS * s + (2 * c + 4))
                for j in range(2):
                    for b in range(PAIR):
                        last = nc.tensor.transpose(back_ps[:, j, b, :], mixed[:, j, b * P:(b + 1) * P], ident[:, :])
                last.then_inc(back_done, 1)

            def stage(l, pair):
                s = 2 * l + pair
                for c in range(CHUNKS):
                    pe.wait_ge(ch_ok, CHUNKS * s + (c + 1))
                    if c == 0:
                        pe.wait_ge(norm_step, NORM_STEPS * (s + 1))
                    if c < CHUNKS - 1:
                        transpose_chunk(c + 1)
                    head(l, s, 2 * c)
                    if c:
                        back(s, c - 1)
                    if c == 3:
                        mean_over_groups(s + 1, False)
                    if c == 5:
                        mean_over_groups(s + 1, True)
                    if c == CHUNKS - 1:
                        pe.wait_ge(norm_step, NORM_STEPS * (s + 1) + FIRST_CHUNK)
                        transpose_chunk(0)
                    head(l, s, 2 * c + 1)
                back(s, CHUNKS - 1)

            pe.sem_inc(head_done, FREE)
            pe.sem_inc(back_done, FREE)
            mean_over_groups(0, False)
            mean_over_groups(0, True)
            pe.wait_ge(norm_step, FIRST_CHUNK)
            transpose_chunk(0)
            pe.wait_ge(zeroed, 4 + 4 * HEADS)
            layers(pe, stage)


_OUT = (BATCH, SEQ, 16, 32)


def kernel(**inputs):
    import numpy as np
    import concourse.bacc as bacc
    from concourse.bass_utils import run_bass_kernel_spmd

    a = {k: np.asarray(v) for k, v in inputs.items()}
    w1, w3, w2 = a["L0_conv_w1"], a["L0_conv_w3"], a["L0_conv_w2"]
    w13T = np.stack([w.transpose(0, 2, 1).reshape(E, KD, P, F) for w in (w1, w3)], axis=3)
    w2T = w2.transpose(0, 2, 1).reshape(E, KF, P, D).transpose(0, 2, 1, 3)
    gate_wT = a["L0_conv_gate_w"].T.reshape(KD, P, E).transpose(1, 0, 2)
    taps = np.zeros((P, LAYERS, HEADS, TAPS), np.float32)
    mixT = np.zeros((P, LAYERS, 2, HD), np.float32)
    for l in range(LAYERS):
        filters = [a[f"L{l + 1}_conv_w{k}"] for k in SCALES]
        for v in range(2):
            mixT[32 * v:32 * v + HEAD_IN, l, v, :] = a[f"L{l + 1}_conv_w_mix"].T
        for h in range(HEADS):
            row0 = head_place(h)[1]
            for m in range(HEAD_IN):
                scale, channel = divmod(HEAD_IN * h + m, D)
                taps[row0 + m, l, h, 0:SCALES[scale]] = filters[scale][channel, 0, ::-1]
    arrays = {"x": a["x"], "gate_wT": gate_wT, "w13T": w13T, "w2T": w2T, "taps": taps, "mixT": mixT}
    arrays = {f"in_{k}": np.ascontiguousarray(v) for k, v in arrays.items()}

    nc = bacc.Bacc("TRN2", target_bir_lowering=False, num_devices=1)
    args = [nc.dram_tensor(k, v.shape, mybir.dt.from_np(v.dtype), kind="ExternalInput").ap() for k, v in arrays.items()]
    out = nc.dram_tensor("out", _OUT, mybir.dt.float32, kind="ExternalOutput").ap()
    build(nc, *args, out)
    return run_bass_kernel_spmd(nc, [arrays], core_ids=[0]).results[0]["out"]
```

```python
import concourse.bass as bass
from concourse import mybir
from contextlib import ExitStack

P = 128
BATCH, SEQ, D, F, E = 4, 512, 512, 1024, 8
QUARTERS = SEQ // P
TILES = BATCH * QUARTERS
TOKENS = BATCH * SEQ
TOP_K = 2
KD = D // P
KF = F // P
GROUP = SEQ // 32
GROUP_LANES = GROUP // QUARTERS
EPS = 1e-5
MAX_BLOCKS = (TOP_K * TOKENS + E * (P - 1)) // P
STRIDE = 2
META = 4
ROW = D + META
LOW = -3.0e38
FREE = 1

LAYERS, HEADS, HD = 3, 16, 32
SCALES = (3, 7, 15)
HEAD_IN = len(SCALES) * HD
PHASES = QUARTERS
PAIR = 2
PT = PAIR * QUARTERS
LEAD = 4
CHUNK_STARTS = [0, 128, 256, 64, 192, 448, 384, 320]
CHUNKS = len(CHUNK_STARTS)
XW = D + 64


def head_place(h):
    start = HEAD_IN * h % D
    begin = start // P * P if start % P <= P - HEAD_IN else (start - 64) // P * P + 64
    return CHUNK_STARTS.index(begin), start - begin


def head_taps(h):
    return SCALES[min((HEAD_IN * h + HEAD_IN - 1) // D, 2)]


CHUNK_HEADS = [[h for h in range(HEADS) if head_place(h)[0] == c] for c in range(CHUNKS)]
ORDER = [h for hs in CHUNK_HEADS for h in hs]
MIX_AT, _at = {}, 0
for _h in range(HEADS):
    MIX_AT[_h] = _at
    _at += (head_taps(_h) + 2 * (PHASES - 1)) * HD
MIX_COLS = _at
TAPS = max(SCALES)
MIX_MAX = TAPS * HD
EARLY = 6


def build(nc, x, gate_wT, w13T, w2T, taps, mixT, out):
    f32, f32r, i32, u32 = mybir.dt.float32, mybir.dt.float32r, mybir.dt.int32, mybir.dt.uint32
    ALU, ACT, AX = mybir.AluOpType, mybir.ActivationFunctionType, mybir.AxisListType

    slots_x = nc.dram_tensor("slots_x", [(MAX_BLOCKS + 1 + E) * P, ROW], f32).ap()
    acc = nc.dram_tensor("acc", [TOKENS + P, D], f32).ap()
    with ExitStack() as ctx:
        def sb(name, shape):
            return ctx.enter_context(nc.sbuf_tensor(name, shape, f32))

        ident = sb("ident", [P, P])
        group_mean = sb("group_mean", [P, P])
        taps_sb = sb("taps_sb", [P, LAYERS + 1, HEADS, TAPS])
        mix_sb = sb("mix_sb", [P, LAYERS + 1, 2, HD])
        taps_in = ctx.enter_context(nc.semaphore("taps_in"))
        experts_part(nc, x, gate_wT, w13T, w2T, slots_x, acc, ident, group_mean, taps, mixT, taps_sb, mix_sb, taps_in)
        conv_part(nc, acc, out, ident, group_mean, taps_sb, mix_sb, taps_in)


def wait_apart(eng, semaphore, value, counter):
    eng.wait_ge(semaphore, value)
    eng.sem_inc(counter, 1)


def experts_part(nc, x, gate_wT, w13T, w2T, slots_x, acc, ident, group_mean, taps, mixT, taps_sb, mix_sb, taps_in):
    f32, f32r, i32, u32 = mybir.dt.float32, mybir.dt.float32r, mybir.dt.int32, mybir.dt.uint32
    ALU, ACT, AX = mybir.AluOpType, mybir.ActivationFunctionType, mybir.AxisListType
    x_rows = x.rearrange("b (p q) h w -> b p q (h w)", q=QUARTERS)

    with ExitStack() as ctx:
        def sb(name, shape, dt=f32):
            return ctx.enter_context(nc.sbuf_tensor(name, shape, dt))

        def ps(name, shape):
            return ctx.enter_context(nc.psum_tensor(name, shape, f32))

        def sem(name):
            return ctx.enter_context(nc.semaphore(name))

        w13_raw = sb("w13_raw", [P, KD, 2, F])
        w13_hi = sb("w13_hi", [P, KD, 2, F], f32r)
        w13_lo = sb("w13_lo", [P, KD, 2, F], f32r)
        w2_raw = sb("w2_raw", [P, KF, D])
        w2_hi = sb("w2_hi", [P, KF, D], f32r)
        w2_lo = sb("w2_lo", [P, KF, D], f32r)
        rows = sb("rows", [P, TILES, ROW])
        block_row = sb("block_row", [P, D])
        logits_T = block_row[0:E, :]
        xT_hi = sb("xT_hi", [P, KD, P], f32r)
        xT_lo = sb("xT_lo", [P, KD, P], f32r)
        silu = sb("silu", [P, F])
        hidden = sb("hidden", [P, F])
        hT_hi = sb("hT_hi", [P, KF, P], f32r)
        hT_lo = sb("hT_lo", [P, KF, P], f32r)
        y_row = sb("y_row", [P, ROW])
        meta = sb("meta", [P, META])
        my_slot = sb("my_slot", [P, 1])
        weight = sb("weight", [P, 1])
        gate_sb = sb("gate_sb", [P, KD, E])
        early_w2 = w2_raw[:, :, :].rearrange("p k n -> p (k n)")
        gate_xT = early_w2.rearrange("p (s k n) -> p s k n", s=2, k=KD)
        place = early_w2.rearrange("p (g i s) -> p g i s", g=2, s=P)
        pad_row = y_row[:, :]
        bn = sb("bn", [P, BATCH, QUARTERS, 6])
        mv = sb("mv", [P, BATCH, 2])
        gmv = sb("gmv", [P, BATCH, 2])
        dev = sb("dev", [P, BATCH, 2])
        rstd = sb("rstd", [P, BATCH, 4])
        ids = sb("ids", [P, TILES], i32)
        pad_id = sb("pad_id", [P, 1], i32)
        rev = sb("rev", [P, E])
        thresholds = sb("thresholds", [P, TILES])
        eq, score, pick1, pick2, lg2, mask, slot = (
            hidden[:, n * P:(n + 1) * P].rearrange("p (i e) -> p i e", e=E) for n in range(7))
        both_picks, both_slots = (hidden[:, n * P:(n + 2) * P].rearrange("p (j i e) -> p j i e", j=TOP_K, e=E) for n in (2, 0))
        restart, totals, running = (
            silu[:, n * P:(n + 1) * P].rearrange("p (e i) -> p e i", i=TILES) for n in range(3))
        from_here, ones, slot_row = (silu[:, n * P:(n + 1) * P] for n in range(3, 6))
        best = silu[:, 6 * P:7 * P].rearrange("p (n i) -> p n i", n=8)
        over = silu[:, 7 * P:8 * P].rearrange("p (e n) -> p e n", e=E)
        nblocks = sb("nblocks", [P, 4, E])
        slot_id = sb("slot_id", [P, TOP_K, TILES], i32)
        table = sb("table", [1, E + 3], i32)
        spans = sb("spans", [P, 3, TILES // STRIDE])
        spare = sb("spare", [P, E])
        pad_slot = sb("pad_slot", [P, 3, E + 1])
        pad_slot_id = sb("pad_slot_id", [P, E + 1], i32)

        xT_ps = ps("xT_ps", [P, 512])
        gate_ps = ps("gate_ps", [P, 2, 512])
        up_ps = ps("up_ps", [P, 2, 512])
        hT_ps = ps("hT_ps", [P, KF, P])
        y_ps = ps("y_ps", [P, 512])

        def logits_bank(b):
            return up_ps[:, 0, :] if b == BATCH - 1 else y_ps

        gate_banks = [gate_ps[:, n, :] for n in range(2)] + [
            hT_ps[:, n * 4:n * 4 + 4, :].rearrange("p k n -> p (k n)") for n in range(2)]

        x_in = [sem(f"x_in{b}") for b in range(BATCH)]
        gate_in = sem("gate_in")
        acc_ready = sem("acc_ready")
        consts = sem("consts")
        pool_step = sem("pool_step")
        d_step = sem("d_step")
        averaged = sem("averaged")
        stat_ps = sem("stat_ps")
        centred = sem("centred")
        rooted = sem("rooted")
        normed = sem("normed")
        gxT_ps = sem("gxT_ps")
        gxT_sb = sem("gxT_sb")
        gate_done = sem("gate_done")
        logits_T_ok = sem("logits_T_ok")
        logits = sem("logits")
        ranks = sem("ranks")
        mask_ready = sem("mask_ready")
        gap_ready = sem("gap_ready")
        exped = sem("exped")
        table_ready = sem("table_ready")
        running_ready = sem("running_ready")
        spans_ready = sem("spans_ready")
        pad_slots_ready = sem("pad_slots_ready")
        pads_in = sem("pads_in")
        rows_ready = sem("rows_ready")
        place_ok = sem("place_ok")
        scattered = sem("scattered")
        w13_in = [sem(f"w13_in{k}") for k in range(KD)]
        w2_in = [sem(f"w2_in{k}") for k in range(2)]
        w13_hi_ok = sem("w13_hi_ok")
        w13_ok = sem("w13_ok")
        w2_hi_ok = sem("w2_hi_ok")
        w2_ok = sem("w2_ok")
        row_in = sem("row_in")
        xT_done = sem("xT_done")
        xT_hi_ok = sem("xT_hi_ok")
        xT_ok = sem("xT_ok")
        up_done = sem("up_done")
        silu_ok = sem("silu_ok")
        hidden_ok = sem("hidden_ok")
        hT_done = sem("hT_done")
        hT_hi_ok = sem("hT_hi_ok")
        hT_ok = sem("hT_ok")
        down_done = sem("down_done")
        y_ok = sem("y_ok")
        meta_in = sem("meta_in")
        weight_ok = sem("weight_ok")
        w_step = sem("w_step")
        added = sem("added")
        passed = sem("passed")

        block = ctx.enter_context(nc.Block(name="experts"))

        def load_w13(eng, e, k):
            eng.dma_start(w13_raw[:, k], w13T[bass.ds(e, 1), k].rearrange("o p t n -> (o p) t n"))\
               .then_inc(w13_in[k], 16)

        def load_w2(eng, e, half):
            k = slice(half * KF // 2, (half + 1) * KF // 2)
            eng.dma_start(w2_raw[:, k], w2T[bass.ds(e, 1), :, k].rearrange("o p t n -> (o p) t n"))\
               .then_inc(w2_in[half], 16)

        def last_block_of(eng, e):
            return eng.value_load(table[0:1, bass.ds(e, 1)], min_val=0, max_val=MAX_BLOCKS - 1)

        def all_blocks(eng, new_expert, body, after_first):
            def one_expert(e, first):
                if not isinstance(e, int):
                    new_expert(e, first)
                body(e, first, True)
                after_first(e, first)
                last = last_block_of(eng, e)
                with eng.If(last > first):
                    with eng.Fori(first + 1, last + 1) as g:
                        body(e, g, False)
            one_expert(0, 0)
            with eng.Fori(1, E) as e:
                one_expert(e, last_block_of(eng, e - 1) + 1)

        @block.sync
        def _(sp):
            for b in range(BATCH):
                sp.dma_start(rows[:, b * QUARTERS:(b + 1) * QUARTERS, 0:D], x_rows[b]).then_inc(x_in[b], 16)
            for k in range(KD):
                load_w13(sp, 0, k)
            for half in range(2):
                sp.wait_ge(xT_done, half + 1)
                load_w2(sp, 0, half)
            sp.wait_ge(row_in, 16)
            sp.wait_ge(pads_in, 16 * (E + 1))
            sp.dma_start(taps_sb[:, 0:LAYERS], taps).then_inc(taps_in, 16)
            sp.dma_start(mix_sb[:, 0:LAYERS], mixT).then_inc(taps_in, 16)
            with sp.Fori(1, E) as e:
                for k in range(KD):
                    sp.wait_ge(w13_ok, (e - 1) * KD + k + 1)
                    if k >= 2:
                        sp.wait_ge(w13_in[k - 2], 16 * (e + 1))
                    load_w13(sp, e, k)
                for half in range(2):
                    sp.wait_ge(w2_ok, (e - 1) * 2 + half + 1)
                    sp.wait_ge(w13_in[KD - 2 + half], 16 * (e + 1))
                    load_w2(sp, e, half)

        @block.gpsimd
        def _(pool):
            steps = [0]

            def step(ins):
                steps[0] += 1
                ins.then_inc(pool_step, 1)
                pool.wait_ge(pool_step, steps[0])

            step(nc.gpsimd.memset(ident[:, :], 0.0))
            step(nc.gpsimd.affine_select(out=ident[:, :], in_=ident[:, :], compare_op=ALU.not_equal, fill=1.0,
                                         base=0, pattern=[[-1, P]], channel_multiplier=1))
            step(nc.gpsimd.memset(group_mean[:, :], 1.0 / GROUP_LANES))
            blocks = group_mean[:, :].rearrange("p (a c) -> p a c", c=GROUP_LANES)
            step(nc.gpsimd.affine_select(out=blocks, in_=blocks, compare_op=ALU.is_ge, fill=0.0, base=0,
                                         pattern=[[-GROUP_LANES, P // GROUP_LANES], [0, GROUP_LANES]],
                                         channel_multiplier=1))
            step(nc.gpsimd.affine_select(out=blocks, in_=blocks, compare_op=ALU.is_ge, fill=0.0,
                                         base=GROUP_LANES - 1,
                                         pattern=[[GROUP_LANES, P // GROUP_LANES], [0, GROUP_LANES]],
                                         channel_multiplier=-1))
            nc.gpsimd.memset(ones, 1.0).then_inc(consts, 1)
            step(nc.gpsimd.memset(from_here, 1.0))
            step(nc.gpsimd.affine_select(out=from_here, in_=from_here, compare_op=ALU.is_ge, fill=0.0,
                                         base=0, pattern=[[-1, P]], channel_multiplier=1))
            step(nc.gpsimd.memset(pad_row, 0.0))
            step(nc.gpsimd.memset(pad_row[:, D + 1:D + 2], -1.0))
            step(nc.gpsimd.iota(pad_id[:, :], pattern=[[0, 1]], base=TOKENS, channel_multiplier=1))
            step(nc.gpsimd.tensor_copy(pad_row[:, D:D + 1].bitcast(i32), pad_id[:, :]))
            step(nc.gpsimd.iota(ids[:, :].rearrange("p (b q) -> p b q", q=QUARTERS),
                                pattern=[[SEQ, BATCH], [1, QUARTERS]], base=0, channel_multiplier=QUARTERS))
            step(nc.gpsimd.iota(rev[:, :], pattern=[[-1, E]], base=E, channel_multiplier=0,
                                allow_small_or_imprecise_dtypes=True))
            step(nc.gpsimd.iota(thresholds[:, :], pattern=[[P, TILES]], base=0, channel_multiplier=0,
                                allow_small_or_imprecise_dtypes=True))
            step(nc.gpsimd.memset(thresholds[:, 0:1], -1.0))
            step(nc.gpsimd.iota(slot_row, pattern=[[1, P]], base=0, channel_multiplier=0,
                                allow_small_or_imprecise_dtypes=True))
            step(nc.gpsimd.iota(my_slot[:, :], pattern=[[0, 1]], base=0, channel_multiplier=1,
                                allow_small_or_imprecise_dtypes=True))
            step(nc.gpsimd.iota(spare[:, :], pattern=[[P, E]], base=(MAX_BLOCKS + 1) * P, channel_multiplier=1,
                                allow_small_or_imprecise_dtypes=True))
            step(nc.gpsimd.memset(restart[:, :, :], 1.0))
            nc.gpsimd.memset(restart[:, :, 0:1], 0.0).then_inc(consts, 1)
            pool.wait_ge(w13_in[KD - 1], 16)
            pool.dma_start(acc[0:TOKENS, :].rearrange("(p a) n -> p (a n)", p=P),
                           x.rearrange("b (p a) h w -> (b p) (a h w)", a=TOKENS // P)).then_inc(acc_ready, 16)
            pool.dma_start(acc[TOKENS:TOKENS + P, :], pad_row[:, 0:D]).then_inc(acc_ready, 16)

            pool.wait_ge(running_ready, 1)
            behind_group = running[:, 0, STRIDE - 1:TILES:STRIDE]
            for n, (op, bound) in enumerate(((ALU.is_lt, P), (ALU.is_le, P), (ALU.is_lt, 2 * P))):
                step(nc.gpsimd.tensor_scalar(spans[:, n, :], behind_group, float(bound), None, op))
            width = TILES // STRIDE
            while width > 1:
                width //= 2
                step(nc.gpsimd.tensor_tensor(spans[:, :, 0:width], spans[:, :, 0:width], spans[:, :, width:2 * width], ALU.add))
            step(nc.gpsimd.tensor_scalar(spans[:, 1, 1:2], nblocks[:, 0, 0:1], 1.0, None, ALU.is_gt))
            step(nc.gpsimd.tensor_tensor(spans[:, 1, 0:1], spans[:, 1, 0:1], spans[:, 1, 1:2], ALU.mult))
            nc.gpsimd.tensor_copy(table[0:1, E:E + 3], spans[0:1, :, 0]).then_inc(spans_ready, 1)
            pool.wait_ge(rows_ready, 1)
            for j in range(TOP_K):
                for i in range(TILES):
                    pool.indirect_dma_start(
                        out=slots_x[:, :], out_offset=bass.IndirectOffsetOnAxis(slot_id[:, j, i:i + 1].bitcast(u32), 0),
                        in_=rows[:, i, :], in_offset=None).then_inc(scattered, 16)

            def pad(e):
                pool.indirect_dma_start(
                    out=slots_x[:, :], out_offset=bass.IndirectOffsetOnAxis(pad_slot_id[:, e:e + 1].bitcast(u32), 0),
                    in_=pad_row, in_offset=None).then_inc(pads_in, 16)

            pool.wait_ge(pad_slots_ready, 1)
            for e in range(3):
                pad(e)
            pool.wait_ge(scattered, 16 * TOP_K * TILES)
            pool.wait_ge(pads_in, 16 * 3)
            pool.dma_start(block_row[:, :], slots_x[2 * P:3 * P, 0:D]).then_inc(row_in, 16)
            for e in range(3, E + 1):
                pad(e)
            pool.wait_ge(pads_in, 16 * (E + 1))
            pool.wait_ge(xT_done, 3)
            pool.dma_start(block_row[:, :], slots_x[3 * P:4 * P, 0:D]).then_inc(row_in, 16)
            pool.wait_ge(acc_ready, 32)

            def add_block(g):
                wait_apart(pool, y_ok, g + 1 + FREE, passed)
                pool.indirect_dma_start(
                    out=acc[:, :], out_offset=bass.IndirectOffsetOnAxis(meta[:, 0:1].bitcast(u32), 0),
                    in_=y_row[:, 0:D], in_offset=None, compute_op=ALU.add).then_inc(added, 16)
                wait_apart(pool, added, 16 * (g + 1), passed)

            def weigh_block(g):
                pool.dma_start(meta[:, :], slots_x[bass.ds(g * P, P), D:ROW]).then_inc(meta_in, 16)
                wait_apart(pool, meta_in, 16 * (g + 1), passed)
                nc.gpsimd.tensor_scalar(weight[:, :], meta[:, 1:2], my_slot[:, :], meta[:, 3:4],
                                        ALU.is_equal, ALU.mult).then_inc(w_step, 1)
                wait_apart(pool, w_step, 2 * g + 1, passed)
                nc.gpsimd.tensor_scalar(my_slot[:, :], my_slot[:, :], float(P), None, ALU.add).then_inc(w_step, 1)
                nc.gpsimd.tensor_tensor(weight[:, :], weight[:, :], meta[:, 2:3], ALU.add).then_inc(weight_ok, 1)
                wait_apart(pool, w_step, 2 * g + 2, passed)
                wait_apart(pool, weight_ok, g + 1, passed)

            def body(e, g, first):
                if isinstance(g, int):
                    return
                with pool.If(g > 2):
                    pool.wait_ge(xT_done, g + 1)
                    pool.dma_start(block_row[:, :], slots_x[bass.ds((g + 1) * P, P), 0:D]).then_inc(row_in, 16)
                with pool.If(g > 1):
                    add_block(g - 2)
                weigh_block(g - 1)

            all_blocks(pool, lambda e, g: None, body, lambda e, g: None)
            g = last_block_of(pool, E - 1)
            add_block(g - 1)
            weigh_block(g)
            add_block(g)
            pool.wait_ge(row_in, 16 * g)

        @block.scalar
        def _(act):
            act.sem_inc(y_ok, FREE)
            act.dma_start(gate_sb[:, :, :], gate_wT).then_inc(gate_in, 16)

            def root(b):
                act.wait_ge(rooted, 2 * b + 1)
                nc.scalar.activation(rstd[:, b, 1:2], rstd[:, b, 0:1], ACT.Sqrt).then_inc(rooted, 1)

            def copy_gate_xT(b):
                if b >= 2:
                    act.wait_ge(gate_done, b - 1)
                for k in range(KD):
                    act.wait_ge(gxT_ps, KD * b + k + 1)
                    nc.scalar.activation(gate_xT[:, b % 2, k, :], gate_banks[k], ACT.Copy).then_inc(gxT_sb, 1)

            def copy_logits_T(b):
                act.wait_ge(gate_done, b + 1)
                if b:
                    act.wait_ge(logits, b)
                nc.scalar.activation(logits_T, xT_ps[0:E, :], ACT.Copy).then_inc(logits_T_ok, 1)

            for b in range(BATCH):
                root(b)
                if b:
                    copy_logits_T(b - 1)
                copy_gate_xT(b)
            copy_logits_T(BATCH - 1)
            act.wait_ge(gap_ready, 1)
            nc.scalar.activation(best[:, 3, :], best[:, 2, :], ACT.Exp).then_inc(exped, 1)

            def split_w13(e, g0):
                for k in range(KD):
                    act.wait_ge(w13_in[k], 16 * (e + 1))
                    if not isinstance(e, int):
                        act.wait_ge(up_done, g0 * KD + (k + 1 - KD))
                    nc.scalar.activation(w13_hi[:, k], w13_raw[:, k], ACT.Copy).then_inc(w13_hi_ok, 1)

            def split_w2(e, g0):
                if not isinstance(e, int):
                    act.wait_ge(down_done, g0 + FREE)
                for half in range(2):
                    act.wait_ge(w2_in[half], 16 * (e + 1))
                    k = slice(half * KF // 2, (half + 1) * KF // 2)
                    nc.scalar.activation(w2_hi[:, k], w2_raw[:, k], ACT.Copy).then_inc(w2_hi_ok, 1)

            def xT_high(g):
                act.wait_ge(xT_done, g + 1)
                nc.scalar.activation(xT_hi[:, :, :].rearrange("p a n -> p (a n)"), xT_ps[:, :], ACT.Copy).then_inc(xT_hi_ok, 1)

            def hT_high(g):
                act.wait_ge(hT_done, g + 1)
                act.wait_ge(down_done, g + FREE)
                nc.scalar.activation(hT_hi[:, :, :], hT_ps[:, :, :], ACT.Copy).then_inc(hT_hi_ok, 1)

            def weigh_y(g):
                act.wait_ge(down_done, g + 1 + FREE)
                act.wait_ge(weight_ok, g + 1)
                nc.scalar.activation(y_row[:, 0:D], y_ps[:, :], ACT.Copy, scale=weight[:, :]).then_inc(y_ok, 1)

            def body(e, g, first):
                if not isinstance(g, int):
                    with act.If(g > 1):
                        weigh_y(g - 2)
                    hT_high(g - 1)
                act.wait_ge(up_done, KD * (g + 1))
                if not isinstance(g, int):
                    act.wait_ge(hidden_ok, g)
                nc.scalar.activation(silu[:, :].rearrange("p (a n) -> p a n", a=2), gate_ps[:, :, :], ACT.Silu).then_inc(silu_ok, 1)
                xT_high(g + 1)

            act.wait_ge(table_ready, 1)
            split_w13(0, 0)
            xT_high(0)
            all_blocks(act, split_w13, body, split_w2)
            g = last_block_of(act, E - 1)
            weigh_y(g - 1)
            hT_high(g)
            weigh_y(g)

        @block.vector
        def _(dve):
            steps = [0]

            def step(ins):
                steps[0] += 1
                ins.then_inc(d_step, 1)
                dve.wait_ge(d_step, steps[0])

            def flush():
                dve.wait_ge(d_step, steps[0])

            def count(ins):
                steps[0] += 1
                ins.then_inc(d_step, 1)

            def lane_statistics(b):
                dve.wait_ge(x_in[b], 16)
                for q in range(QUARTERS):
                    count(nc.vector.bn_stats(bn[:, b, q, :], rows[:, b * QUARTERS + q, 0:D]))
                flush()
                nc.vector.bn_aggr(mv[:, b, :], bn[:, b, :, :].rearrange("p q s -> p (q s)")).then_inc(averaged, 1)

            def deviation(b):
                dve.wait_ge(stat_ps, 2 * b + 1)
                step(nc.vector.tensor_copy(gmv[:, b, :], up_ps[:, 0, 2 * b:2 * b + 2]))
                step(nc.vector.tensor_scalar(dev[:, b, 0:1], mv[:, b, 0:1], gmv[:, b, 0:1], None, ALU.subtract))
                nc.vector.tensor_tensor(dev[:, b, 1:2], dev[:, b, 0:1], dev[:, b, 0:1], ALU.mult).then_inc(centred, 1)

            def variance(b):
                dve.wait_ge(stat_ps, 2 * b + 2)
                nc.vector.tensor_scalar(rstd[:, b, 0:1], up_ps[:, 1, b:b + 1], gmv[:, b, 1:2], EPS, ALU.add, ALU.add).then_inc(rooted, 1)

            def normalise(b):
                dve.wait_ge(rooted, 2 * b + 2)
                step(nc.vector.reciprocal(rstd[:, b, 2:3], rstd[:, b, 1:2]))
                r = rows[:, b * QUARTERS:(b + 1) * QUARTERS, 0:D]
                nc.vector.tensor_scalar(r, r, gmv[:, b, 0:1], rstd[:, b, 2:3], ALU.subtract, ALU.mult).then_inc(normed, 1)

            for b in range(BATCH):
                lane_statistics(b)
                deviation(b)
                variance(b)
                normalise(b)

            dve.wait_ge(consts, 2)
            def pick(source, top, which, onehot, t):
                bc = [P, t.stop - t.start, E]
                step(nc.vector.tensor_reduce(best[:, top, t], source[:, t], axis=AX.X, op=ALU.max))
                step(nc.vector.tensor_tensor(eq[:, t, :], source[:, t], best[:, top, t, None].to_broadcast(bc), ALU.is_equal))
                step(nc.vector.tensor_tensor(score[:, t, :], eq[:, t, :], rev[:, None, :].to_broadcast(bc), ALU.mult))
                step(nc.vector.tensor_reduce(best[:, which, t], score[:, t, :], axis=AX.X, op=ALU.max))
                step(nc.vector.tensor_tensor(onehot[:, t], score[:, t, :], best[:, which, t, None].to_broadcast(bc), ALU.is_equal))

            for first_batch, end_batch in ((0, BATCH - 1), (BATCH - 1, BATCH)):
                dve.wait_ge(logits, end_batch)
                t = slice(first_batch * QUARTERS, end_batch * QUARTERS)
                lg = logits_bank(first_batch)[:, 0:TILES * E].rearrange("p (i e) -> p i e", e=E)
                pick(lg, 0, 6, pick1, t)
                step(nc.vector.scalar_tensor_tensor(lg2[:, t, :], pick1[:, t, :], LOW, lg[:, t], ALU.mult, ALU.add))
                pick(lg2, 1, 7, pick2, t)
                nc.vector.tensor_tensor(mask[:, t, :], pick1[:, t, :], pick2[:, t, :], ALU.add).then_inc(mask_ready, 1)
            nc.vector.tensor_tensor(best[:, 2, :], best[:, 1, :], best[:, 0, :], ALU.subtract).then_inc(gap_ready, 1)
            dve.wait_ge(exped, 1)
            step(nc.vector.tensor_scalar(best[:, 4, :], best[:, 3, :], 1.0, None, ALU.add))
            step(nc.vector.reciprocal(best[:, 5, :], best[:, 4, :]))
            step(nc.vector.tensor_tensor(rows[:, :, D + 2], best[:, 3, :], best[:, 5, :], ALU.mult))
            count(nc.vector.tensor_tensor(rows[:, :, D + 3], best[:, 5, :], rows[:, :, D + 2], ALU.subtract))
            count(nc.vector.tensor_copy(rows[:, :, D].bitcast(i32), ids[:, :]))
            dve.wait_ge(ranks, 2)
            step(nc.vector.tensor_copy(totals[:, :, :], hT_ps[:, 4, :].rearrange("p (i e) -> p e i", e=E)))
            step(nc.vector.tensor_tensor_scan(running[:, :, :].rearrange("p e i -> p (e i)"),
                                              restart[:, :, :].rearrange("p e i -> p (e i)"),
                                              totals[:, :, :].rearrange("p e i -> p (e i)"), 0.0, ALU.mult, ALU.add))
            step(nc.vector.tensor_tensor(over[:, :, :], running[:, :, TILES - 1:TILES].to_broadcast([P, E, TILES]),
                                         thresholds[:, None, :].to_broadcast([P, E, TILES]), ALU.is_gt))
            step(nc.vector.tensor_reduce(nblocks[:, 0, :], over[:, :, :], axis=AX.X, op=ALU.add))
            step(nc.vector.tensor_tensor_scan(nblocks[:, 1, :], ones[:, 0:E], nblocks[:, 0, :], 0.0, ALU.mult, ALU.add))
            step(nc.vector.tensor_tensor(nblocks[:, 2, :], nblocks[:, 1, :], nblocks[:, 0, :], ALU.subtract))
            nc.vector.tensor_scalar(table[0:1, 0:E], nblocks[0:1, 1, :], 1.0, None, ALU.subtract).then_inc(table_ready, 1)
            step(nc.vector.tensor_scalar(nblocks[:, 3, :], nblocks[:, 2, :], float(P), None, ALU.mult))
            step(nc.vector.tensor_tensor(running[:, :, :], running[:, :, :], nblocks[:, 3, :, None].to_broadcast([P, E, TILES]), ALU.add))
            dve.sem_inc(running_ready, 1)
            step(nc.vector.tensor_tensor(slot[:, :, :], running[:, :, :].rearrange("p e i -> p i e"),
                                         hT_ps[:, 0, :].rearrange("p (i e) -> p i e", e=E), ALU.subtract))
            step(nc.vector.tensor_tensor(both_slots, slot[:, None, :, :].to_broadcast([P, TOP_K, TILES, E]), both_picks, ALU.mult))
            step(nc.vector.tensor_reduce(best[:, 6:8, :], both_slots, axis=AX.X, op=ALU.add))
            count(nc.vector.tensor_copy(slot_id[:, :, :], best[:, 6:8, :]))
            count(nc.vector.tensor_copy(rows[:, :, D + 1], best[:, 6, :]))
            flush()
            dve.sem_inc(rows_ready, 1)

            def find_places(g, slots):
                nc.vector.tensor_tensor(place[:, g], slot_row[:, None, :].to_broadcast([P, TILES, P]),
                                        slots[:, :, None].to_broadcast([P, TILES, P]), ALU.is_equal).then_inc(place_ok, 1)

            step(nc.vector.tensor_tensor(best[:, 4, :], best[:, 6, :], best[:, 7, :], ALU.min))
            find_places(0, best[:, 4, :])

            def block_1_and_pads():
                step(nc.vector.tensor_scalar(best[:, 0:2, :], best[:, 6:8, :], float(P), -LOW, ALU.is_lt, ALU.mult))
                step(nc.vector.tensor_tensor(best[:, 0:2, :], best[:, 0:2, :], best[:, 6:8, :], ALU.add))
                step(nc.vector.tensor_tensor(best[:, 2, :], best[:, 0, :], best[:, 1, :], ALU.min))
                step(nc.vector.tensor_scalar(best[:, 2, :], best[:, 2, :], float(P), None, ALU.subtract))
                find_places(1, best[:, 2, :])
                behind, beyond, shift = (pad_slot[:, n, 0:E] for n in range(3))
                step(nc.vector.tensor_scalar(behind, running[:, :, TILES - 1], my_slot[:, :], None, ALU.add))
                step(nc.vector.scalar_tensor_tensor(beyond, nblocks[:, 1, :], float(P), behind, ALU.mult, ALU.is_le))
                step(nc.vector.tensor_tensor(shift, spare[:, :], behind, ALU.subtract))
                step(nc.vector.tensor_tensor(shift, shift, beyond, ALU.mult))
                step(nc.vector.tensor_tensor(behind, behind, shift, ALU.add))
                step(nc.vector.tensor_scalar(pad_slot[:, 0, E:E + 1], nblocks[:, 1, E - 1:E], float(P), my_slot[:, :], ALU.mult, ALU.add))
                nc.vector.tensor_copy(pad_slot_id[:, :], pad_slot[:, 0, :]).then_inc(pad_slots_ready, 1)

            def split_w13(e, g0, chunks=range(KD)):
                for k in chunks:
                    dve.wait_ge(w13_hi_ok, KD * e + (k + 1))
                    nc.vector.tensor_tensor(w13_lo[:, k], w13_raw[:, k], w13_hi[:, k].bitcast(f32),
                                            ALU.subtract).then_inc(w13_ok, 1)

            def split_w2(e, g0):
                for half in range(2):
                    dve.wait_ge(w2_hi_ok, 2 * e + (half + 1))
                    k = slice(half * KF // 2, (half + 1) * KF // 2)
                    nc.vector.tensor_tensor(w2_lo[:, k], w2_raw[:, k], w2_hi[:, k].bitcast(f32),
                                            ALU.subtract).then_inc(w2_ok, 1)

            def xT_low(g):
                dve.wait_ge(xT_hi_ok, g + 1)
                nc.vector.tensor_tensor(xT_lo[:, :, :].rearrange("p a n -> p (a n)"), xT_ps[:, :],
                                        xT_hi[:, :, :].rearrange("p a n -> p (a n)").bitcast(f32), ALU.subtract).then_inc(xT_ok, 1)

            def hT_low(g):
                dve.wait_ge(hT_hi_ok, g + 1)
                nc.vector.tensor_tensor(hT_lo[:, :, :], hT_ps[:, :, :], hT_hi[:, :, :].bitcast(f32),
                                        ALU.subtract).then_inc(hT_ok, 1)

            def body(e, g, first):
                if not isinstance(g, int):
                    hT_low(g - 1)
                dve.wait_ge(silu_ok, g + 1)
                if not isinstance(g, int):
                    dve.wait_ge(hT_done, g)
                nc.vector.tensor_tensor(hidden[:, :].rearrange("p (a n) -> p a n", a=2),
                                        silu[:, :].rearrange("p (a n) -> p a n", a=2), up_ps[:, :, :],
                                        ALU.mult).then_inc(hidden_ok, 1)
                xT_low(g + 1)

            split_w13(0, 0, range(KD // 2))
            block_1_and_pads()
            xT_low(0)
            split_w13(0, 0, range(KD // 2, KD))
            all_blocks(dve, split_w13, body, split_w2)
            hT_low(last_block_of(dve, E - 1))

        @block.tensor
        def _(pe):
            pe.sem_inc(down_done, FREE)
            pe.wait_ge(pool_step, 5)

            def group_means(b):
                pe.wait_ge(averaged, b + 1)
                nc.tensor.matmul(up_ps[:, 0, 2 * b:2 * b + 2], group_mean[:, :], mv[:, b, :], start=True, stop=True).then_inc(stat_ps, 1)

            def group_deviation(b):
                pe.wait_ge(centred, b + 1)
                nc.tensor.matmul(up_ps[:, 1, b:b + 1], group_mean[:, :], dev[:, b, 1:2], start=True, stop=True).then_inc(stat_ps, 1)

            def transpose_batch(b):
                pe.wait_ge(normed, b + 1)
                for k in range(KD):
                    if b:
                        pe.wait_ge(gxT_sb, KD * (b - 1) + k + 1)
                    for q in range(QUARTERS):
                        last = nc.tensor.transpose(gate_banks[k][:, q * P:(q + 1) * P],
                                                   rows[:, b * QUARTERS + q, k * P:(k + 1) * P], ident[:, :])
                    last.then_inc(gxT_ps, 1)

            def gate_product(b, chunks):
                if b and 0 in chunks:
                    pe.wait_ge(logits_T_ok, b)
                for k in chunks:
                    pe.wait_ge(gxT_sb, KD * b + k + 1)
                    last = nc.tensor.matmul(xT_ps[0:E, :], gate_sb[:, k, :], gate_xT[:, b % 2, k, :],
                                            start=(k == 0), stop=(k == KD - 1))
                if KD - 1 in chunks:
                    last.then_inc(gate_done, 1)

            def transpose_logits(b):
                pe.wait_ge(logits_T_ok, b + 1)
                for q in range(QUARTERS):
                    i = b * QUARTERS + q
                    last = nc.tensor.transpose(logits_bank(b)[:, i * E:(i + 1) * E], logits_T[:, q * P:(q + 1) * P], ident[0:E, 0:E])
                last.then_inc(logits, 1)

            group_means(0)
            group_deviation(0)
            pe.wait_ge(gate_in, 16)
            for b in range(BATCH):
                transpose_batch(b)
                if b:
                    transpose_logits(b - 1)
                gate_product(b, [0])
                if b + 1 < BATCH:
                    group_means(b + 1)
                gate_product(b, [1])
                if b + 1 < BATCH:
                    group_deviation(b + 1)
                gate_product(b, range(2, KD))
            transpose_logits(BATCH - 1)
            pe.wait_ge(mask_ready, 2)
            pe.wait_ge(consts, 1)
            pe.wait_ge(pool_step, 7)
            nc.tensor.matmul(hT_ps[:, 0, :], from_here, mask[:, :, :].rearrange("p i e -> p (i e)"), start=True, stop=True).then_inc(ranks, 1)
            nc.tensor.matmul(hT_ps[:, 4, :], ones, mask[:, :, :].rearrange("p i e -> p (i e)"), start=True, stop=True).then_inc(ranks, 1)

            pe.wait_ge(spans_ready, 1)
            end_0, first_1, end_1 = (
                pe.value_load(table[0:1, E + n:E + n + 1], min_val=0, max_val=TILES // STRIDE) for n in range(3))

            def gather(g, begin, end):
                pe.wait_ge(place_ok, g + 1)
                if g:
                    pe.wait_ge(xT_ok, g)

                def nothing(start):
                    return nc.tensor.matmul(xT_ps[:, 0:P], rows[0:1, 0, 0:P], pad_row[0:1, 0:P], start=start, stop=not start)

                def group_of_tiles(n):
                    for i in range(n * STRIDE, (n + 1) * STRIDE):
                        for k in range(KD):
                            nc.tensor.matmul(xT_ps[:, k * P:(k + 1) * P], rows[:, i, k * P:(k + 1) * P], place[:, g, i, :],
                                             start=False, stop=False)

                nothing(True)
                for n in range(TILES // STRIDE):
                    if n == 0 and begin is None:
                        group_of_tiles(n)
                    elif n == 0:
                        with pe.If(begin < 1):
                            group_of_tiles(n)
                    elif begin is None:
                        with pe.If(end > n - 1):
                            group_of_tiles(n)
                    else:
                        with pe.If(end > n - 1):
                            with pe.If(begin < n + 1):
                                group_of_tiles(n)
                nothing(False).then_inc(xT_done, 1)

            def next_rows(g):
                pe.wait_ge(row_in, 16 * g)
                for k in range(KD):
                    last = nc.tensor.transpose(xT_ps[:, k * P:(k + 1) * P], block_row[:, k * P:(k + 1) * P], ident[:, :])
                last.then_inc(xT_done, 1)

            def down(g, w2_count):
                pe.wait_ge(y_ok, g + FREE)
                pe.wait_ge(w2_ok, w2_count)
                pe.wait_ge(hT_hi_ok, g + 1)
                for k in range(KF):
                    for b in (w2_hi, w2_lo):
                        nc.tensor.matmul(y_ps[:, :], hT_hi[:, k, :], b[:, k, :], start=(k == 0 and b is w2_hi), stop=False)
                pe.wait_ge(hT_ok, g + 1)
                for k in range(KF):
                    last = nc.tensor.matmul(y_ps[:, :], hT_lo[:, k, :], w2_hi[:, k, :], start=False, stop=(k == KF - 1))
                last.then_inc(down_done, 1)

            def body(e, g, first):
                pe.wait_ge(xT_ok, g + 1)
                for k in range(KD):
                    pe.wait_ge(w13_ok, KD * e + (k + 1))
                    for a, b in ((xT_hi, w13_hi), (xT_hi, w13_lo), (xT_lo, w13_hi)):
                        for t, o in ((0, gate_ps), (1, up_ps)):
                            for n in range(2):
                                last = nc.tensor.matmul(o[:, n, :], a[:, k, :], b[:, k, t, n * 512:(n + 1) * 512],
                                                        start=(k == 0 and a is xT_hi and b is w13_hi),
                                                        stop=(k == KD - 1 and a is xT_lo))
                    last.then_inc(up_done, 1)
                if isinstance(g, int):
                    gather(1, first_1, end_1)
                else:
                    next_rows(g)
                if not isinstance(g, int):
                    down(g - 1, 2 * e if first else 2 * e + 2)
                pe.wait_ge(hidden_ok, g + 1)
                for k in range(KF):
                    last = nc.tensor.transpose(hT_ps[:, k, :], hidden[:, k * P:(k + 1) * P], ident[:, :])
                last.then_inc(hT_done, 1)

            pe.wait_ge(table_ready, 1)
            gather(0, None, end_0)
            all_blocks(pe, lambda e, g: None, body, lambda e, g: None)
            down(last_block_of(pe, E - 1), 2 * E)



def conv_part(nc, acc, out, ident, group_mean, taps_sb, mix_sb, taps_in):
    f32, f32r = mybir.dt.float32, mybir.dt.float32r
    ALU, ACT = mybir.AluOpType, mybir.ActivationFunctionType
    acc_rows = acc[0:TOKENS, :].rearrange("(b p q) n -> b p q n", p=P, q=QUARTERS)
    out_rows = out.rearrange("b (p q) h w -> b p q (h w)", q=QUARTERS)
    STATS, CENTRED, ROOTED, FIRST_CHUNK, NORM_STEPS = 10, 13, 14, 17, 21

    with ExitStack() as ctx:
        def sb(name, shape, dt=f32):
            return ctx.enter_context(nc.sbuf_tensor(name, shape, dt))

        def ps(name, shape):
            return ctx.enter_context(nc.psum_tensor(name, shape, f32))

        def sem(name):
            return ctx.enter_context(nc.semaphore(name))

        tokens = sb("tokens", [P, TILES, D])
        norm = sb("norm", [P, PT, XW])
        ch_hi = [sb(f"ch_hi{i}", [P, PAIR, QUARTERS, LEAD + P], f32r) for i in range(2)]
        ch_lo = [sb(f"ch_lo{i}", [P, PAIR, QUARTERS, LEAD + P], f32r) for i in range(2)]
        mix_hi = sb("mix_hi", [P, MIX_COLS], f32r)
        mix_lo = sb("mix_lo", [P, MIX_COLS], f32r)
        product = [sb(f"product{i}", [P, MIX_MAX]) for i in range(4)]
        mixed = sb("mixed", [P, 2, PAIR * P])
        bn = sb("bn_c", [P, PAIR, QUARTERS, 6])
        mv = sb("mv_c", [P, PAIR, 2])
        gmv = sb("gmv_c", [P, PAIR, 2])
        dev = sb("dev_c", [P, PAIR])
        dev2 = sb("dev2_c", [P, PAIR])
        var = sb("var_c", [P, PAIR])
        std = sb("std_c", [P, PAIR])
        rstd = sb("rstd_c", [P, PAIR])

        chT_ps = ps("chT_ps", [P, PT, P])
        mixed_ps = [ps(f"mixed_ps{i}", [P, 512]) for i in range(2)]
        back_ps = ps("back_ps", [P, 2, PAIR, P])
        stat_ps = ps("stat_ps", [P, 512])
        stat2_ps = ps("stat2_ps", [P, 512])

        half_in = [sem(f"half_in{i}") for i in range(2 * PAIR)]
        rest_in = sem("rest_in")
        zeroed = sem("zeroed")
        norm_step = sem("norm_step")
        stat_done = sem("stat_done")
        root_ok = sem("root_ok")
        chT_done = sem("chT_done")
        ch_hi_ok = sem("ch_hi_ok")
        ch_ok = sem("ch_ok")
        head_done = sem("head_done")
        mixed_ok = sem("mixed_ok")
        back_done = sem("back_done")
        summed = sem("summed")
        product_ok = sem("product_ok")
        mix_hi_ok = sem("mix_hi_ok")
        mix_ok = sem("mix_ok")
        stored = sem("stored")
        passed = sem("passed_c")
        block = ctx.enter_context(nc.Block(name="convolutions"))

        def middle(t, h):
            at = MIX_AT[h] + (PHASES - 1) * HD
            return t[:, at:at + head_taps(h) * HD]

        @block.sync
        def _(sp):
            for n in range(2 * PAIR):
                b, q = n // 2, n % 2 * 2
                sp.dma_start(tokens[:, 2 * n:2 * n + 2, :], acc_rows[b, :, q:q + 2]).then_inc(half_in[n], 16)
            for b in range(PAIR, BATCH):
                sp.dma_start(tokens[:, b * QUARTERS:(b + 1) * QUARTERS, :], acc_rows[b]).then_inc(rest_in, 16)
            last = CHUNKS * (2 * LAYERS - 1) + FREE
            sp.wait_ge(summed, last)
            for b in range(PAIR):
                sp.dma_start(out_rows[b], tokens[:, b * QUARTERS:(b + 1) * QUARTERS, :]).then_inc(stored, 16)
            late = sorted(h for hs in CHUNK_HEADS[-2:] for h in hs)
            runs = [list(zip([0] + [(h + 1) * HD for h in late], [h * HD for h in late] + [D]))]
            runs += [[(h * HD, (h + 1) * HD) for h in hs] for hs in CHUNK_HEADS[-2:]]
            stores = PAIR
            for chunks, columns in zip((CHUNKS - 2, CHUNKS - 1, CHUNKS), runs):
                sp.wait_ge(summed, last + chunks)
                for b in range(PAIR, BATCH):
                    for begin, end in columns:
                        if begin < end:
                            sp.dma_start(out_rows[b, :, :, begin:end],
                                         tokens[:, b * QUARTERS:(b + 1) * QUARTERS, begin:end]).then_inc(stored, 16)
                            stores += 1
            sp.wait_ge(stored, 16 * stores)

        @block.gpsimd
        def _(pool):
            for i in range(2):
                nc.gpsimd.memset(ch_hi[i][:, :, :, 0:LEAD].bitcast(f32), 0.0).then_inc(zeroed, 1)
                nc.gpsimd.memset(ch_lo[i][:, :, :, 0:LEAD].bitcast(f32), 0.0).then_inc(zeroed, 1)
            for h in ORDER:
                for t in (mix_hi, mix_lo):
                    k = head_taps(h)
                    for at in (MIX_AT[h], MIX_AT[h] + (PHASES - 1 + k) * HD):
                        nc.gpsimd.memset(t[:, at:at + (PHASES - 1) * HD].bitcast(f32), 0.0).then_inc(zeroed, 1)

        def layers(eng, stage):
            with eng.Fori(0, LAYERS) as l:
                for pair in range(2):
                    stage(l, pair)

        @block.scalar
        def _(act):
            def root(s):
                act.wait_ge(norm_step, NORM_STEPS * s + ROOTED)
                nc.scalar.activation(std[:, :], var[:, :], ACT.Sqrt).then_inc(root_ok, 1)

            def high(s, c):
                act.wait_ge(chT_done, CHUNKS * s + (c + 1))
                nc.scalar.activation(ch_hi[c % 2][:, :, :, LEAD:].rearrange("p b q n -> p (b q) n"),
                                     chT_ps[:, :, :], ACT.Copy).then_inc(ch_hi_ok, 1)

            def mix_high(l, o):
                h = ORDER[o]
                act.wait_ge(product_ok, HEADS * l + (o + 1))
                nc.scalar.activation(middle(mix_hi, h), product[o % 4][:, 0:head_taps(h) * HD], ACT.Copy).then_inc(mix_hi_ok, 1)

            def evacuate(s, o):
                act.wait_ge(head_done, HEADS * s + (o + 1) + FREE)
                act.wait_ge(back_done, CHUNKS * s + o // 2 + FREE)
                nc.scalar.activation(mixed[:, o % 2, :], mixed_ps[o % 2][:, 0:PAIR * P], ACT.Copy).then_inc(mixed_ok, 1)

            def stage(l, pair):
                s = 2 * l + pair
                for c in range(CHUNKS):
                    if c < CHUNKS - 1:
                        act.wait_ge(head_done, HEADS * s + 2 * c + FREE)
                        high(s, c + 1)
                    if c == 6:
                        root(s + 1)
                    evacuate(s, 2 * c)
                    if c == CHUNKS - 1:
                        high(s + 1, 0)
                    evacuate(s, 2 * c + 1)
                    if pair == 1 and c >= 1:
                        with act.If(l < LAYERS - 1):
                            mix_high(l + 1, 2 * c - 2)
                            mix_high(l + 1, 2 * c - 1)
                if pair == 1:
                    with act.If(l < LAYERS - 1):
                        mix_high(l + 1, HEADS - 2)
                        mix_high(l + 1, HEADS - 1)

            act.sem_inc(mixed_ok, 2)
            for o in range(EARLY):
                mix_high(0, o)
            root(0)
            high(0, 0)
            for o in range(EARLY, HEADS):
                mix_high(0, o)
            layers(act, stage)

        @block.vector
        def _(dve):
            def stats(s, pair, b):
                for q in range(QUARTERS):
                    if s is None and q % 2 == 0:
                        dve.wait_ge(half_in[2 * b + q // 2], 16)
                    nc.vector.bn_stats(bn[:, b, q, :], tokens[:, pair * PT + b * QUARTERS + q, :]).then_inc(norm_step, 1)

            def aggregate(s):
                wait_apart(dve, norm_step, NORM_STEPS * s + 8, passed)
                for b in range(PAIR):
                    nc.vector.bn_aggr(mv[:, b, :], bn[:, b, :, :].rearrange("p q s -> p (q s)")).then_inc(norm_step, 1)

            def deviate(s):
                dve.wait_ge(stat_done, 2 * s + 1)
                nc.vector.tensor_copy(gmv[:, :, :].rearrange("p b s -> p (b s)"), stat_ps[:, 0:4]).then_inc(norm_step, 1)
                dve.wait_ge(norm_step, NORM_STEPS * s + 11)
                nc.vector.tensor_tensor(dev[:, :], mv[:, :, 0], gmv[:, :, 0], ALU.subtract).then_inc(norm_step, 1)
                dve.wait_ge(norm_step, NORM_STEPS * s + 12)
                nc.vector.tensor_tensor(dev2[:, :], dev[:, :], dev[:, :], ALU.mult).then_inc(norm_step, 1)

            def variance(s):
                dve.wait_ge(stat_done, 2 * s + 2)
                nc.vector.scalar_tensor_tensor(var[:, :], stat2_ps[:, 0:2], EPS, gmv[:, :, 1], ALU.add, ALU.add).then_inc(norm_step, 1)

            def normalise(s, pair):
                dve.wait_ge(root_ok, s + 1)
                nc.vector.reciprocal(rstd[:, :], std[:, :]).then_inc(norm_step, 1)
                dve.wait_ge(norm_step, NORM_STEPS * s + 15)
                dve.wait_ge(chT_done, CHUNKS * s)
                for at, n in ((0, P), (P, D - P), (D, XW - D)):
                    for b in range(PAIR):
                        t0 = b * QUARTERS
                        source = at % D
                        nc.vector.tensor_scalar(norm[:, t0:t0 + QUARTERS, at:at + n],
                                                tokens[:, pair * PT + t0:pair * PT + t0 + QUARTERS, source:source + n],
                                                gmv[:, b, 0:1], rstd[:, b:b + 1], ALU.subtract, ALU.mult).then_inc(norm_step, 1)

            def low(s, c):
                dve.wait_ge(ch_hi_ok, CHUNKS * s + (c + 1))
                nc.vector.tensor_tensor(ch_lo[c % 2][:, :, :, LEAD:].rearrange("p b q n -> p (b q) n"), chT_ps[:, :, :],
                                        ch_hi[c % 2][:, :, :, LEAD:].rearrange("p b q n -> p (b q) n").bitcast(f32),
                                        ALU.subtract).then_inc(ch_ok, 1)

            def add_back(s, pair, c):
                dve.wait_ge(back_done, CHUNKS * s + (c + 1) + FREE)
                for j, h in enumerate(CHUNK_HEADS[c]):
                    t = tokens[:, pair * PT:(pair + 1) * PT, h * HD:(h + 1) * HD]
                    ins = nc.vector.tensor_tensor(t, t, back_ps[:, j, :, :].rearrange("p b (q d) -> p (b q) d", d=HD), ALU.add)
                ins.then_inc(summed, 1)

            def mix_product(l, o):
                h = ORDER[o]
                k = head_taps(h)
                row0 = head_place(h)[1]
                if isinstance(l, int):
                    if o >= 4:
                        dve.wait_ge(mix_ok, HEADS * l + o - 3)
                else:
                    dve.wait_ge(mix_ok, HEADS * l + (o - 3))
                lt = slice(l, l + 1) if isinstance(l, int) else bass.ds(l, 1)
                a = taps_sb[:, lt, h, 0:k].rearrange("p o k -> p (o k)")[:, :, None].to_broadcast([P, k, HD])
                b = mix_sb[:, lt, row0 // 32, :].to_broadcast([P, k, HD])
                nc.vector.tensor_tensor(product[o % 4][:, 0:k * HD].rearrange("p (k d) -> p k d", d=HD), a, b,
                                        ALU.mult).then_inc(product_ok, 1)

            def mix_low(l, o):
                h = ORDER[o]
                dve.wait_ge(mix_hi_ok, HEADS * l + (o + 1))
                nc.vector.tensor_tensor(middle(mix_lo, h), product[o % 4][:, 0:head_taps(h) * HD],
                                        middle(mix_hi, h).bitcast(f32), ALU.subtract).then_inc(mix_ok, 1)

            def stage(l, pair):
                s = 2 * l + pair
                for c in range(CHUNKS):
                    if c == 6:
                        variance(s + 1)
                    if c < CHUNKS - 1:
                        low(s, c + 1)
                    else:
                        low(s + 1, 0)
                    if c == 6:
                        normalise(s + 1, 1 - pair)
                    if c:
                        add_back(s, pair, c - 1)
                    elif pair:
                        add_back(s - 1, 0, CHUNKS - 1)
                    if c < 2:
                        dve.wait_ge(summed, CHUNKS * s + FREE)
                        stats(s + 1, 1 - pair, c)
                    if c == 2:
                        aggregate(s + 1)
                    if c == 4:
                        deviate(s + 1)
                    if pair == 1 and c >= 1:
                        with dve.If(l < LAYERS - 1):
                            mix_product(l + 1, 2 * c - 2)
                            mix_product(l + 1, 2 * c - 1)
                            if c >= 2:
                                mix_low(l + 1, 2 * c - 4)
                                mix_low(l + 1, 2 * c - 3)
                if pair == 1:
                    add_back(s, pair, CHUNKS - 1)
                    with dve.If(l < LAYERS - 1):
                        mix_product(l + 1, HEADS - 2)
                        mix_product(l + 1, HEADS - 1)
                        for o in range(HEADS - 4, HEADS):
                            mix_low(l + 1, o)

            dve.sem_inc(summed, FREE)
            dve.wait_ge(taps_in, 32)
            for o in range(EARLY):
                mix_product(0, o)
                if o >= 3:
                    mix_low(0, o - 3)
            for b in range(PAIR):
                stats(None, 0, b)
            aggregate(0)
            mix_low(0, EARLY - 3)
            deviate(0)
            mix_low(0, EARLY - 2)
            variance(0)
            mix_low(0, EARLY - 1)
            normalise(0, 0)
            low(0, 0)
            for o in range(EARLY, HEADS):
                mix_product(0, o)
                if o >= EARLY + 2:
                    mix_low(0, o - 2)
            mix_low(0, HEADS - 2)
            mix_low(0, HEADS - 1)
            dve.wait_ge(rest_in, 16 * PAIR)
            layers(dve, stage)

        @block.tensor
        def _(pe):
            def mean_over_groups(s, second):
                pe.wait_ge(norm_step, NORM_STEPS * s + (CENTRED if second else STATS))
                if second:
                    ins = nc.tensor.matmul(stat2_ps[:, 0:PAIR], group_mean[:, :], dev2[:, :], start=True, stop=True)
                else:
                    ins = nc.tensor.matmul(stat_ps[:, 0:2 * PAIR], group_mean[:, :], mv[:, :, :].rearrange("p b s -> p (b s)"), start=True, stop=True)
                ins.then_inc(stat_done, 1)

            def transpose_chunk(c):
                at = CHUNK_STARTS[c]
                for i in range(PT):
                    last = nc.tensor.transpose(chT_ps[:, i, :], norm[:, i, at:at + P], ident[:, :])
                last.then_inc(chT_done, 1)

            def head(l, s, o):
                h = ORDER[o]
                k, c = head_taps(h), o // 2
                pe.wait_ge(mix_ok, HEADS * l + (o + 1))
                pe.wait_ge(mixed_ok, HEADS * s + (o + 1))
                res = mixed_ps[o % 2][:, 0:PAIR * P].rearrange("p (b n) -> p b n", b=PAIR)
                shifts = range(-(k - 1), PHASES)
                for r in shifts:
                    a, q = r // PHASES, r % PHASES
                    at = MIX_AT[h] + (PHASES - 1 - r) * HD
                    for w, x in ((mix_hi, ch_hi), (mix_hi, ch_lo), (mix_lo, ch_hi)):
                        last = nc.tensor.matmul(res, w[:, at:at + P], x[c % 2][:, :, q, LEAD + a:LEAD + a + P],
                                                start=(r == shifts[0] and w is mix_hi and x is ch_hi),
                                                stop=(r == shifts[-1] and w is mix_lo))
                last.then_inc(head_done, 1)

            def back(s, c):
                pe.wait_ge(summed, CHUNKS * s + c + FREE)
                pe.wait_ge(mixed_ok, HEADS * s + (2 * c + 4))
                for j in range(2):
                    for b in range(PAIR):
                        last = nc.tensor.transpose(back_ps[:, j, b, :], mixed[:, j, b * P:(b + 1) * P], ident[:, :])
                last.then_inc(back_done, 1)

            def stage(l, pair):
                s = 2 * l + pair
                for c in range(CHUNKS):
                    pe.wait_ge(ch_ok, CHUNKS * s + (c + 1))
                    head(l, s, 2 * c)
                    if c == 0:
                        pe.wait_ge(norm_step, NORM_STEPS * (s + 1))
                    if c < CHUNKS - 1:
                        transpose_chunk(c + 1)
                    if c:
                        back(s, c - 1)
                    elif pair:
                        back(s - 1, CHUNKS - 1)
                    if c == 3:
                        mean_over_groups(s + 1, False)
                    if c == 5:
                        mean_over_groups(s + 1, True)
                    if c == CHUNKS - 1:
                        pe.wait_ge(norm_step, NORM_STEPS * (s + 1) + FIRST_CHUNK)
                        transpose_chunk(0)
                    head(l, s, 2 * c + 1)
                if pair:
                    back(s, CHUNKS - 1)

            pe.sem_inc(head_done, FREE)
            pe.sem_inc(back_done, FREE)
            mean_over_groups(0, False)
            mean_over_groups(0, True)
            pe.wait_ge(norm_step, FIRST_CHUNK)
            transpose_chunk(0)
            pe.wait_ge(zeroed, 4 + 4 * HEADS)
            layers(pe, stage)


_OUT = (BATCH, SEQ, 16, 32)


def kernel(**inputs):
    import numpy as np
    import concourse.bacc as bacc
    from concourse.bass_utils import run_bass_kernel_spmd

    a = {k: np.asarray(v) for k, v in inputs.items()}
    w1, w3, w2 = a["L0_conv_w1"], a["L0_conv_w3"], a["L0_conv_w2"]
    w13T = np.stack([w.transpose(0, 2, 1).reshape(E, KD, P, F) for w in (w1, w3)], axis=3)
    w2T = w2.transpose(0, 2, 1).reshape(E, KF, P, D).transpose(0, 2, 1, 3)
    gate_wT = a["L0_conv_gate_w"].T.reshape(KD, P, E).transpose(1, 0, 2)
    taps = np.zeros((P, LAYERS, HEADS, TAPS), np.float32)
    mixT = np.zeros((P, LAYERS, 2, HD), np.float32)
    for l in range(LAYERS):
        filters = [a[f"L{l + 1}_conv_w{k}"] for k in SCALES]
        for v in range(2):
            mixT[32 * v:32 * v + HEAD_IN, l, v, :] = a[f"L{l + 1}_conv_w_mix"].T
        for h in range(HEADS):
            row0 = head_place(h)[1]
            for m in range(HEAD_IN):
                scale, channel = divmod(HEAD_IN * h + m, D)
                taps[row0 + m, l, h, 0:SCALES[scale]] = filters[scale][channel, 0, ::-1]
    arrays = {"x": a["x"], "gate_wT": gate_wT, "w13T": w13T, "w2T": w2T, "taps": taps, "mixT": mixT}
    arrays = {f"in_{k}": np.ascontiguousarray(v) for k, v in arrays.items()}

    nc = bacc.Bacc("TRN2", target_bir_lowering=False, num_devices=1)
    args = [nc.dram_tensor(k, v.shape, mybir.dt.from_np(v.dtype), kind="ExternalInput").ap() for k, v in arrays.items()]
    out = nc.dram_tensor("out", _OUT, mybir.dt.float32, kind="ExternalOutput").ap()
    build(nc, *args, out)
    return run_bass_kernel_spmd(nc, [arrays], core_ids=[0]).results[0]["out"]
```
